# Optimizing a Trainium2 kernel written in Bass

```python
import numpy as np
import jax
import jax.numpy as jnp

def _softmax(x, axis=-1):
    return jax.nn.softmax(x, axis=axis)

def _gelu(x):
    return jax.nn.gelu(x, approximate=True)

def _silu(x):
    return jax.nn.silu(x)

def _sigmoid(x):
    return jax.nn.sigmoid(x)

def _layernorm(x, axis=-1, eps=1e-05):
    m = jnp.mean(x, axis=axis, keepdims=True)
    v = jnp.var(x, axis=axis, keepdims=True)
    return (x - m) / jnp.sqrt(v + eps)

def _scatter_add(tgt, idx, src, axis=0):
    return tgt.at[idx].add(src)

def _segment_sum(src, seg, n):
    return jax.ops.segment_sum(src, seg, n)
kernel_name = 'mk_perceiver_d2_seqx_r4_be68a6'

def setup_inputs(seed: int=0):
    np.random.seed(seed)
    _w = jnp.asarray

    def _rec_inputs():
        import jax
        import jax.numpy as jnp
        _rk = jax.random.key(seed)
        x = -0.0002928 + 1 * jax.random.normal(jax.random.fold_in(_rk, 1), (16, 64, 256), jnp.float32)
        _lenS = 64 - jax.random.randint(jax.random.fold_in(_rk, 7), (16,), 0, max(1, 64 // 4) + 1, jnp.int32)
        _lenS2 = 1601 - jax.random.randint(jax.random.fold_in(_rk, 8), (16,), 0, max(1, 1601 // 4) + 1, jnp.int32)
        _ctx_1024P = jax.random.normal(jax.random.fold_in(_rk, 11), (16, 16, 256), jnp.float32)
        _ctx_1024c = jax.random.dirichlet(jax.random.fold_in(_rk, 511), 0.3 * jnp.ones((16,), jnp.float32), (16, 1601))
        _ctx_1024t = jnp.einsum('bsk,bkd->bsd', _ctx_1024c, _ctx_1024P)
        _ctx_1024t = _ctx_1024t * jax.lax.rsqrt(jnp.mean(jnp.square(_ctx_1024t)) + 1e-12) * 0.953939
        ctx_1024 = -1.39393e-06 + 0.999914 * (_ctx_1024t + 0.3 * jax.random.normal(jax.random.fold_in(_rk, 611), (16, 1601, 256), jnp.float32))
        _validS = jnp.arange(64)[None, :] < _lenS[:, None]
        _validS2 = jnp.arange(1601)[None, :] < _lenS2[:, None]
        _causal = jnp.tril(jnp.ones((64, 64), dtype=bool))
        mask_BxS2_bf0 = jnp.logical_not(jnp.ones((16, 1601), dtype=bool))
        return (x, ctx_1024, mask_BxS2_bf0)
    x, ctx_1024, mask_BxS2_bf0 = _rec_inputs()

    def _L0_xattn_setup():
        import jax, jax.numpy as jnp
        import numpy as np
        HID = 256
        HEADS = 16
        HEAD_DIM = HID // HEADS
        MAX_REL = 2

        def _rel_embeddings(table, length_q, length_k):
            dist = jnp.arange(length_k)[None, :] - jnp.arange(length_q)[:, None]
            idx = jnp.clip(dist, -MAX_REL, MAX_REL) + MAX_REL
            return table[idx]
        key = jax.random.key(seed)
        ks = jax.random.split(key, 16)
        B, L = (2, 512)
        s = 1.0 / np.sqrt(HID)
        inp = {'query': jax.random.normal(ks[0], (B, L, HID), jnp.float32), 'key': jax.random.normal(ks[1], (B, L, HID), jnp.float32), 'value': jax.random.normal(ks[2], (B, L, HID), jnp.float32), 'Wq': jax.random.normal(ks[3], (HID, HID), jnp.float32) * s, 'bq': jnp.zeros((HID,), jnp.float32), 'Wk': jax.random.normal(ks[4], (HID, HID), jnp.float32) * s, 'bk': jnp.zeros((HID,), jnp.float32), 'Wv': jax.random.normal(ks[5], (HID, HID), jnp.float32) * s, 'bv': jnp.zeros((HID,), jnp.float32), 'Wo': jax.random.normal(ks[6], (HID, HID), jnp.float32) * s, 'bo': jnp.zeros((HID,), jnp.float32), 'rel_k': jax.random.normal(ks[7], (2 * MAX_REL + 1, HEAD_DIM), jnp.float32) * 0.1, 'rel_v': jax.random.normal(ks[8], (2 * MAX_REL + 1, HEAD_DIM), jnp.float32) * 0.1}
        return inp
    _L0_xattn_all = _L0_xattn_setup()
    _L0_xattn_in = {k: v for k, v in _L0_xattn_all.items() if k in ('Wq', 'bq', 'Wk', 'bk', 'Wv', 'bv', 'Wo', 'bo', 'rel_k', 'rel_v')}
    del _L0_xattn_all

    def _L0_attn_setup():
        import jax, jax.numpy as jnp
        import numpy as np
        D_MODEL = 256
        N_HEADS = 16
        HEAD_DIM = D_MODEL // N_HEADS
        KV_LATENT = 64
        LN_EPS = 1e-05

        def apply_rope(x):
            b, h, t, d = x.shape
            half = d // 2
            pos = jnp.arange(t, dtype=x.dtype)[:, None]
            inv_freq = 1.0 / 10000.0 ** (jnp.arange(half, dtype=x.dtype) / half)
            angles = pos * inv_freq[None, :]
            sin = jnp.sin(angles)[None, None]
            cos = jnp.cos(angles)[None, None]
            x1, x2 = (x[..., :half], x[..., half:])
            return jnp.concatenate([x1 * cos - x2 * sin, x1 * sin + x2 * cos], axis=-1)
        key = jax.random.key(seed)
        ks = jax.random.split(key, 6)
        d, L = (D_MODEL, KV_LATENT)
        s = 1.0 / np.sqrt(d)
        sl = 1.0 / np.sqrt(L)
        return {'x': jax.random.normal(ks[0], (2, 512, d), dtype=jnp.float32), 'W_q': jax.random.uniform(ks[1], (d, d), jnp.float32, -s, s), 'W_dkv': jax.random.uniform(ks[2], (d, L), jnp.float32, -s, s), 'W_uk': jax.random.uniform(ks[3], (L, d), jnp.float32, -sl, sl), 'W_uv': jax.random.uniform(ks[4], (L, d), jnp.float32, -sl, sl), 'W_o': jax.random.uniform(ks[5], (d, d), jnp.float32, -s, s), 'ln_gamma': jnp.ones((L,), jnp.float32), 'ln_beta': jnp.zeros((L,), jnp.float32)}
    _L0_attn_all = _L0_attn_setup()
    _L0_attn_in = {k: v for k, v in _L0_attn_all.items() if k in ('W_q', 'W_dkv', 'W_uk', 'W_uv', 'W_o', 'ln_gamma', 'ln_beta')}
    del _L0_attn_all

    def _L0_ffn_setup():
        import jax, jax.numpy as jnp
        import numpy as np
        QMAX = 127.0

        def _quant_dequant(w):
            scale = jnp.max(jnp.abs(w), axis=-1, keepdims=True) / QMAX
            scale = jnp.maximum(scale, 1e-08)
            q = jnp.clip(jnp.round(w / scale), -QMAX, QMAX)
            return q * scale
        key = jax.random.key(seed)
        ks = jax.random.split(key, 7)
        B, S, D, F, E, NS = (2, 512, 256, 512, 8, 1)
        std = 1.0 / np.sqrt(D)
        x = jax.random.normal(ks[0], (B, S, D), dtype=jnp.float32)
        router_w = _quant_dequant(jax.random.normal(ks[1], (E, D), dtype=jnp.float32) * std)
        router_b = jnp.zeros((E,), dtype=jnp.float32)
        w_up = _quant_dequant(jax.random.normal(ks[2], (E, F, D), dtype=jnp.float32) * std)
        w_down = _quant_dequant(jax.random.normal(ks[3], (E, D, F), dtype=jnp.float32) / np.sqrt(F))
        shared_w_up = _quant_dequant(jax.random.normal(ks[4], (NS, F, D), dtype=jnp.float32) * std)
        shared_w_down = _quant_dequant(jax.random.normal(ks[5], (NS, D, F), dtype=jnp.float32) / np.sqrt(F))
        return {'x': x, 'router_w': router_w, 'router_b': router_b, 'w_up': w_up, 'w_down': w_down, 'shared_w_up': shared_w_up, 'shared_w_down': shared_w_down}
    _L0_ffn_all = _L0_ffn_setup()
    _L0_ffn_in = {k: v for k, v in _L0_ffn_all.items() if k in ('router_w', 'router_b', 'w_up', 'w_down', 'shared_w_up', 'shared_w_down')}
    del _L0_ffn_all

    def _L1_xattn_setup():
        import jax, jax.numpy as jnp
        import numpy as np
        B, SQ, SKV, D, H = (2, 512, 512, 256, 16)
        HD = D // H

        def cross_attention(query, context, mask, Wq, bq, Wkv, bkv, Wout, bout, num_heads):
            b, sq, d = query.shape
            skv = context.shape[1]
            hd = d // num_heads
            scale = hd ** (-0.5)
            q = query @ Wq + bq
            kv = context @ Wkv + bkv
            kv = kv.reshape(b, skv, 2, num_heads, hd).transpose(2, 0, 3, 1, 4)
            k, v = (kv[0], kv[1])
            q = q.reshape(b, sq, num_heads, hd).transpose(0, 2, 1, 3)
            scores = jnp.einsum('bhid,bhjd->bhij', q, k) * scale
            scores = jnp.where(mask[:, None, None, :], -jnp.inf, scores)
            attn = jax.nn.softmax(scores, axis=-1)
            out = jnp.einsum('bhij,bhjd->bhid', attn, v)
            out = out.transpose(0, 2, 1, 3).reshape(b, sq, d)
            return out @ Wout + bout
        key = jax.random.key(seed)
        ks = jax.random.split(key, 6)
        scale = 1.0 / np.sqrt(D)
        return {'query': jax.random.normal(ks[0], (B, SQ, D), dtype=jnp.float32), 'context': jax.random.normal(ks[1], (B, SKV, D), dtype=jnp.float32), 'mask': jnp.zeros((B, SKV), dtype=bool), 'Wq': jax.random.normal(ks[2], (D, D), dtype=jnp.float32) * scale, 'bq': jnp.zeros((D,), dtype=jnp.float32), 'Wkv': jax.random.normal(ks[3], (D, 2 * D), dtype=jnp.float32) * scale, 'bkv': jnp.zeros((2 * D,), dtype=jnp.float32), 'Wout': jax.random.normal(ks[4], (D, D), dtype=jnp.float32) * scale, 'bout': jnp.zeros((D,), dtype=jnp.float32), 'num_heads': H}
    _L1_xattn_all = _L1_xattn_setup()
    _L1_xattn_in = {k: v for k, v in _L1_xattn_all.items() if k in ('Wq', 'bq', 'Wkv', 'bkv', 'Wout', 'bout')}
    del _L1_xattn_all

    def _L1_attn_setup():
        import jax, jax.numpy as jnp
        import numpy as np
        D, H, DK, DV, F, R = (256, 16, 64, 64, 1024, 64)
        B, T = (4, 512)
        KCONV = 4
        EPS = 1e-06

        def rmsnorm(x, w):
            return x * jax.lax.rsqrt(jnp.mean(x * x, axis=-1, keepdims=True) + EPS) * w

        def _reference_tuple_inner(x, norm_in_w, conv_w, conv_b, q_w, k_w, v_w, out_w, alpha_w, alpha_b, beta_w, beta_b, head_norm_w, u1_w, u1_b, u2_w, u2_b, ff_norm_w, ff_w1, ff_w3, ff_w2):
            bsz, seq, _ = x.shape
            h = rmsnorm(x, norm_in_w)
            hc = jax.lax.conv_general_dilated(h.transpose(0, 2, 1), conv_w, (1,), [(KCONV - 1, 0)], dimension_numbers=('NCH', 'OIH', 'NCH'), feature_group_count=D)
            h = jax.nn.silu((hc + conv_b[None, :, None]).transpose(0, 2, 1))
            q = (h @ q_w).reshape(bsz, seq, H, DK)
            k = (h @ k_w).reshape(bsz, seq, H, DK)
            v = (h @ v_w).reshape(bsz, seq, H, DV)
            q = q / (jnp.linalg.norm(q, axis=-1, keepdims=True) + EPS)
            k = k / (jnp.linalg.norm(k, axis=-1, keepdims=True) + EPS)
            alpha = jax.nn.sigmoid(h @ alpha_w + alpha_b).reshape(bsz, seq, H, DK)
            beta = jax.nn.sigmoid(h @ beta_w + beta_b)

            def step(s, inp):
                qt, kt, vt, at, bt = inp
                s = s * at[..., None]
                u = jnp.einsum('bhd,bhdv->bhv', kt, s)
                s = s + bt[..., None, None] * (kt[..., None] * (vt - u)[..., None, :])
                out = jnp.einsum('bhdv,bhd->bhv', s, qt)
                return (s, out)
            tm = lambda a: jnp.swapaxes(a, 0, 1)
            s0 = jnp.zeros((bsz, H, DK, DV), x.dtype)
            s_final, outs = jax.lax.scan(step, s0, (tm(q), tm(k), tm(v), tm(alpha), tm(beta)))
            y = tm(outs)
            y = y * jax.lax.rsqrt(jnp.mean(y * y, axis=-1, keepdims=True) + EPS) * head_norm_w
            y = y.reshape(bsz, seq, H * DV)
            gate = jax.nn.sigmoid(jax.nn.silu(x @ u1_w + u1_b) @ u2_w + u2_b)
            y = x + y @ out_w * gate
            y2 = rmsnorm(y, ff_norm_w)
            y = y + jax.nn.silu(y2 @ ff_w1) * (y2 @ ff_w3) @ ff_w2
            return (y, s_final)
        key = jax.random.key(seed)
        ks = jax.random.split(key, 16)
        n = lambda k, shape: jax.random.normal(k, shape, jnp.float32) * 0.02
        return dict(x=jax.random.normal(ks[0], (B, T, D), jnp.float32), norm_in_w=jnp.ones((D,), jnp.float32), conv_w=n(ks[1], (D, 1, KCONV)), conv_b=jnp.zeros((D,), jnp.float32), q_w=n(ks[2], (D, H * DK)), k_w=n(ks[3], (D, H * DK)), v_w=n(ks[4], (D, H * DV)), out_w=n(ks[5], (H * DV, D)), alpha_w=n(ks[6], (D, H * DK)), alpha_b=jnp.zeros((H * DK,), jnp.float32), beta_w=n(ks[7], (D, H)), beta_b=jnp.zeros((H,), jnp.float32), head_norm_w=jnp.ones((H, DV), jnp.float32), u1_w=n(ks[8], (D, R)), u1_b=jnp.zeros((R,), jnp.float32), u2_w=n(ks[9], (R, D)), u2_b=jnp.zeros((D,), jnp.float32), ff_norm_w=jnp.ones((D,), jnp.float32), ff_w1=n(ks[10], (D, F)), ff_w3=n(ks[11], (D, F)), ff_w2=n(ks[12], (F, D)))
    _L1_attn_all = _L1_attn_setup()
    _L1_attn_in = {k: v for k, v in _L1_attn_all.items() if k in ('norm_in_w', 'conv_w', 'conv_b', 'q_w', 'k_w', 'v_w', 'out_w', 'alpha_w', 'alpha_b', 'beta_w', 'beta_b', 'head_norm_w', 'u1_w', 'u1_b', 'u2_w', 'u2_b', 'ff_norm_w', 'ff_w1', 'ff_w3', 'ff_w2')}
    del _L1_attn_all

    def _L1_ffn_setup():
        import jax, jax.numpy as jnp
        import numpy as np
        BLOCK = 16
        _GRID = jnp.array([0.0, 0.5, 1.0, 1.5, 2.0, 3.0, 4.0, 6.0], dtype=jnp.float32)
        _MID = jnp.array([0.25, 0.75, 1.25, 1.75, 2.5, 3.5, 5.0], dtype=jnp.float32)

        def fp4_quant_dequant(x):
            shape = x.shape
            xb = x.reshape(shape[:-1] + (shape[-1] // BLOCK, BLOCK))
            scale = jnp.max(jnp.abs(xb), axis=-1, keepdims=True) / 6.0
            scale = jnp.maximum(scale, jnp.float32(1e-12))
            xn = xb / scale
            idx = jnp.searchsorted(_MID, jnp.abs(xn))
            q = _GRID[idx] * jnp.sign(xn) * scale
            return q.reshape(shape)

        def fp4_linear(x, w):
            xq = fp4_quant_dequant(x)
            wq = fp4_quant_dequant(w)
            return jnp.einsum('bsk,nk->bsn', xq, wq)
        key = jax.random.key(seed)
        k1, k2, k3, k4 = jax.random.split(key, 4)
        H, I = (256, 704)
        x = jax.random.normal(k1, (4, 1024, H), dtype=jnp.float32)
        w_gate = jax.random.normal(k2, (I, H), dtype=jnp.float32) * 0.02
        w_up = jax.random.normal(k3, (I, H), dtype=jnp.float32) * 0.02
        w_down = jax.random.normal(k4, (H, I), dtype=jnp.float32) * 0.02
        return {'x': x, 'w_gate': w_gate, 'w_up': w_up, 'w_down': w_down}
    _L1_ffn_all = _L1_ffn_setup()
    _L1_ffn_in = {k: v for k, v in _L1_ffn_all.items() if k in ('w_gate', 'w_up', 'w_down')}
    del _L1_ffn_all
    return {'x': x, 'ctx_1024': ctx_1024, 'mask_BxS2_bf0': mask_BxS2_bf0, 'L0_xattn_Wq': _L0_xattn_in['Wq'], 'L0_xattn_bq': _L0_xattn_in['bq'], 'L0_xattn_Wk': _L0_xattn_in['Wk'], 'L0_xattn_bk': _L0_xattn_in['bk'], 'L0_xattn_Wv': _L0_xattn_in['Wv'], 'L0_xattn_bv': _L0_xattn_in['bv'], 'L0_xattn_Wo': _L0_xattn_in['Wo'], 'L0_xattn_bo': _L0_xattn_in['bo'], 'L0_xattn_rel_k': _L0_xattn_in['rel_k'], 'L0_xattn_rel_v': _L0_xattn_in['rel_v'], 'L0_attn_W_q': _L0_attn_in['W_q'], 'L0_attn_W_dkv': _L0_attn_in['W_dkv'], 'L0_attn_W_uk': _L0_attn_in['W_uk'], 'L0_attn_W_uv': _L0_attn_in['W_uv'], 'L0_attn_W_o': _L0_attn_in['W_o'], 'L0_attn_ln_gamma': _L0_attn_in['ln_gamma'], 'L0_attn_ln_beta': _L0_attn_in['ln_beta'], 'L0_ffn_router_w': _L0_ffn_in['router_w'], 'L0_ffn_router_b': _L0_ffn_in['router_b'], 'L0_ffn_w_up': _L0_ffn_in['w_up'], 'L0_ffn_w_down': _L0_ffn_in['w_down'], 'L0_ffn_shared_w_up': _L0_ffn_in['shared_w_up'], 'L0_ffn_shared_w_down': _L0_ffn_in['shared_w_down'], 'L1_xattn_Wq': _L1_xattn_in['Wq'], 'L1_xattn_bq': _L1_xattn_in['bq'], 'L1_xattn_Wkv': _L1_xattn_in['Wkv'], 'L1_xattn_bkv': _L1_xattn_in['bkv'], 'L1_xattn_Wout': _L1_xattn_in['Wout'], 'L1_xattn_bout': _L1_xattn_in['bout'], 'L1_attn_norm_in_w': _L1_attn_in['norm_in_w'], 'L1_attn_conv_w': _L1_attn_in['conv_w'], 'L1_attn_conv_b': _L1_attn_in['conv_b'], 'L1_attn_q_w': _L1_attn_in['q_w'], 'L1_attn_k_w': _L1_attn_in['k_w'], 'L1_attn_v_w': _L1_attn_in['v_w'], 'L1_attn_out_w': _L1_attn_in['out_w'], 'L1_attn_alpha_w': _L1_attn_in['alpha_w'], 'L1_attn_alpha_b': _L1_attn_in['alpha_b'], 'L1_attn_beta_w': _L1_attn_in['beta_w'], 'L1_attn_beta_b': _L1_attn_in['beta_b'], 'L1_attn_head_norm_w': _L1_attn_in['head_norm_w'], 'L1_attn_u1_w': _L1_attn_in['u1_w'], 'L1_attn_u1_b': _L1_attn_in['u1_b'], 'L1_attn_u2_w': _L1_attn_in['u2_w'], 'L1_attn_u2_b': _L1_attn_in['u2_b'], 'L1_attn_ff_norm_w': _L1_attn_in['ff_norm_w'], 'L1_attn_ff_w1': _L1_attn_in['ff_w1'], 'L1_attn_ff_w3': _L1_attn_in['ff_w3'], 'L1_attn_ff_w2': _L1_attn_in['ff_w2'], 'L1_ffn_w_gate': _L1_ffn_in['w_gate'], 'L1_ffn_w_up': _L1_ffn_in['w_up'], 'L1_ffn_w_down': _L1_ffn_in['w_down']}

def reference(x, ctx_1024, mask_BxS2_bf0, L0_xattn_Wq, L0_xattn_bq, L0_xattn_Wk, L0_xattn_bk, L0_xattn_Wv, L0_xattn_bv, L0_xattn_Wo, L0_xattn_bo, L0_xattn_rel_k, L0_xattn_rel_v, L0_attn_W_q, L0_attn_W_dkv, L0_attn_W_uk, L0_attn_W_uv, L0_attn_W_o, L0_attn_ln_gamma, L0_attn_ln_beta, L0_ffn_router_w, L0_ffn_router_b, L0_ffn_w_up, L0_ffn_w_down, L0_ffn_shared_w_up, L0_ffn_shared_w_down, L1_xattn_Wq, L1_xattn_bq, L1_xattn_Wkv, L1_xattn_bkv, L1_xattn_Wout, L1_xattn_bout, L1_attn_norm_in_w, L1_attn_conv_w, L1_attn_conv_b, L1_attn_q_w, L1_attn_k_w, L1_attn_v_w, L1_attn_out_w, L1_attn_alpha_w, L1_attn_alpha_b, L1_attn_beta_w, L1_attn_beta_b, L1_attn_head_norm_w, L1_attn_u1_w, L1_attn_u1_b, L1_attn_u2_w, L1_attn_u2_b, L1_attn_ff_norm_w, L1_attn_ff_w1, L1_attn_ff_w3, L1_attn_ff_w2, L1_ffn_w_gate, L1_ffn_w_up, L1_ffn_w_down):
    import jax
    import jax.numpy as jnp

    def _L0_xattn_ref(query, key, value, Wq, bq, Wk, bk, Wv, bv, Wo, bo, rel_k, rel_v):
        import jax, jax.numpy as jnp
        import numpy as np
        HID = 256
        HEADS = 16
        HEAD_DIM = HID // HEADS
        MAX_REL = 2

        def _rel_embeddings(table, length_q, length_k):
            dist = jnp.arange(length_k)[None, :] - jnp.arange(length_q)[:, None]
            idx = jnp.clip(dist, -MAX_REL, MAX_REL) + MAX_REL
            return table[idx]
        B, Lq, _ = query.shape
        Lk = key.shape[1]
        q = query @ Wq + bq
        k = key @ Wk + bk
        v = value @ Wv + bv
        qh = q.reshape(B, Lq, HEADS, HEAD_DIM).transpose(0, 2, 1, 3)
        kh = k.reshape(B, Lk, HEADS, HEAD_DIM).transpose(0, 2, 1, 3)
        vh = v.reshape(B, Lk, HEADS, HEAD_DIM).transpose(0, 2, 1, 3)
        attn1 = jnp.einsum('bhqd,bhkd->bhqk', qh, kh)
        rk = _rel_embeddings(rel_k, Lq, Lk)
        attn2 = jnp.einsum('bhqd,qkd->bhqk', qh, rk)
        scale = jnp.sqrt(jnp.asarray(HEAD_DIM, query.dtype))
        attn = jax.nn.softmax((attn1 + attn2) / scale, axis=-1)
        w1 = jnp.einsum('bhqk,bhkd->bhqd', attn, vh)
        rv = _rel_embeddings(rel_v, Lq, Lk)
        w2 = jnp.einsum('bhqk,qkd->bhqd', attn, rv)
        x = (w1 + w2).transpose(0, 2, 1, 3).reshape(B, Lq, HID)
        return x @ Wo + bo

    def _L0_attn_ref(x, W_q, W_dkv, W_uk, W_uv, W_o, ln_gamma, ln_beta):
        import jax, jax.numpy as jnp
        import numpy as np
        D_MODEL = 256
        N_HEADS = 16
        HEAD_DIM = D_MODEL // N_HEADS
        KV_LATENT = 64
        LN_EPS = 1e-05

        def apply_rope(x):
            b, h, t, d = x.shape
            half = d // 2
            pos = jnp.arange(t, dtype=x.dtype)[:, None]
            inv_freq = 1.0 / 10000.0 ** (jnp.arange(half, dtype=x.dtype) / half)
            angles = pos * inv_freq[None, :]
            sin = jnp.sin(angles)[None, None]
            cos = jnp.cos(angles)[None, None]
            x1, x2 = (x[..., :half], x[..., half:])
            return jnp.concatenate([x1 * cos - x2 * sin, x1 * sin + x2 * cos], axis=-1)
        b, t, _ = x.shape
        q = (x @ W_q).reshape(b, t, N_HEADS, HEAD_DIM).transpose(0, 2, 1, 3)
        lat = x @ W_dkv
        mu = jnp.mean(lat, axis=-1, keepdims=True)
        var = jnp.mean(jnp.square(lat - mu), axis=-1, keepdims=True)
        lat = (lat - mu) * jax.lax.rsqrt(var + LN_EPS) * ln_gamma + ln_beta
        k = (lat @ W_uk).reshape(b, t, N_HEADS, HEAD_DIM).transpose(0, 2, 1, 3)
        v = (lat @ W_uv).reshape(b, t, N_HEADS, HEAD_DIM).transpose(0, 2, 1, 3)
        q = apply_rope(q)
        k = apply_rope(k)
        scores = jnp.einsum('bhqd,bhkd->bhqk', q, k) / jnp.sqrt(jnp.float32(HEAD_DIM))
        causal = jnp.tril(jnp.ones((t, t), dtype=bool))
        scores = jnp.where(causal[None, None], scores, -jnp.inf)
        attn = jax.nn.softmax(scores, axis=-1)
        out = jnp.einsum('bhqk,bhkd->bhqd', attn, v)
        out = out.transpose(0, 2, 1, 3).reshape(b, t, D_MODEL)
        return out @ W_o

    def _L0_ffn_ref(x, router_w, router_b, w_up, w_down, shared_w_up, shared_w_down):
        import jax, jax.numpy as jnp
        import numpy as np
        QMAX = 127.0

        def _quant_dequant(w):
            scale = jnp.max(jnp.abs(w), axis=-1, keepdims=True) / QMAX
            scale = jnp.maximum(scale, 1e-08)
            q = jnp.clip(jnp.round(w / scale), -QMAX, QMAX)
            return q * scale
        B, S, D = x.shape
        E = router_w.shape[0]
        TOPK = 2
        xt = x.reshape(-1, D)
        logits = xt @ router_w.T + router_b
        probs = jax.nn.softmax(logits, axis=-1)
        top_vals, top_idx = jax.lax.top_k(probs, TOPK)
        top_vals = top_vals / jnp.sum(top_vals, axis=-1, keepdims=True)
        combine = jnp.sum(jax.nn.one_hot(top_idx, E, dtype=xt.dtype) * top_vals[..., None], axis=1)
        h = jnp.einsum('td,efd->tef', xt, w_up)
        y = jnp.einsum('tef,edf->ted', jax.nn.silu(h), w_down)
        out = jnp.einsum('ted,te->td', y, combine)
        hs = jnp.einsum('td,sfd->tsf', xt, shared_w_up)
        out = out + jnp.einsum('tsf,sdf->td', jax.nn.silu(hs), shared_w_down)
        return out.reshape(B, S, D)

    def _L1_xattn_ref(query, context, mask, Wq, bq, Wkv, bkv, Wout, bout, num_heads):
        import jax, jax.numpy as jnp
        import numpy as np
        B, SQ, SKV, D, H = (2, 512, 512, 256, 16)
        HD = D // H

        def cross_attention(query, context, mask, Wq, bq, Wkv, bkv, Wout, bout, num_heads):
            b, sq, d = query.shape
            skv = context.shape[1]
            hd = d // num_heads
            scale = hd ** (-0.5)
            q = query @ Wq + bq
            kv = context @ Wkv + bkv
            kv = kv.reshape(b, skv, 2, num_heads, hd).transpose(2, 0, 3, 1, 4)
            k, v = (kv[0], kv[1])
            q = q.reshape(b, sq, num_heads, hd).transpose(0, 2, 1, 3)
            scores = jnp.einsum('bhid,bhjd->bhij', q, k) * scale
            scores = jnp.where(mask[:, None, None, :], -jnp.inf, scores)
            attn = jax.nn.softmax(scores, axis=-1)
            out = jnp.einsum('bhij,bhjd->bhid', attn, v)
            out = out.transpose(0, 2, 1, 3).reshape(b, sq, d)
            return out @ Wout + bout
        return cross_attention(query, context, mask, Wq, bq, Wkv, bkv, Wout, bout, num_heads)

    def _L1_attn_ref(x, norm_in_w, conv_w, conv_b, q_w, k_w, v_w, out_w, alpha_w, alpha_b, beta_w, beta_b, head_norm_w, u1_w, u1_b, u2_w, u2_b, ff_norm_w, ff_w1, ff_w3, ff_w2):
        import jax, jax.numpy as jnp
        import numpy as np
        D, H, DK, DV, F, R = (256, 16, 64, 64, 1024, 64)
        B, T = (4, 512)
        KCONV = 4
        EPS = 1e-06

        def rmsnorm(x, w):
            return x * jax.lax.rsqrt(jnp.mean(x * x, axis=-1, keepdims=True) + EPS) * w

        def _reference_tuple_inner(x, norm_in_w, conv_w, conv_b, q_w, k_w, v_w, out_w, alpha_w, alpha_b, beta_w, beta_b, head_norm_w, u1_w, u1_b, u2_w, u2_b, ff_norm_w, ff_w1, ff_w3, ff_w2):
            bsz, seq, _ = x.shape
            h = rmsnorm(x, norm_in_w)
            hc = jax.lax.conv_general_dilated(h.transpose(0, 2, 1), conv_w, (1,), [(KCONV - 1, 0)], dimension_numbers=('NCH', 'OIH', 'NCH'), feature_group_count=D)
            h = jax.nn.silu((hc + conv_b[None, :, None]).transpose(0, 2, 1))
            q = (h @ q_w).reshape(bsz, seq, H, DK)
            k = (h @ k_w).reshape(bsz, seq, H, DK)
            v = (h @ v_w).reshape(bsz, seq, H, DV)
            q = q / (jnp.linalg.norm(q, axis=-1, keepdims=True) + EPS)
            k = k / (jnp.linalg.norm(k, axis=-1, keepdims=True) + EPS)
            alpha = jax.nn.sigmoid(h @ alpha_w + alpha_b).reshape(bsz, seq, H, DK)
            beta = jax.nn.sigmoid(h @ beta_w + beta_b)

            def step(s, inp):
                qt, kt, vt, at, bt = inp
                s = s * at[..., None]
                u = jnp.einsum('bhd,bhdv->bhv', kt, s)
                s = s + bt[..., None, None] * (kt[..., None] * (vt - u)[..., None, :])
                out = jnp.einsum('bhdv,bhd->bhv', s, qt)
                return (s, out)
            tm = lambda a: jnp.swapaxes(a, 0, 1)
            s0 = jnp.zeros((bsz, H, DK, DV), x.dtype)
            s_final, outs = jax.lax.scan(step, s0, (tm(q), tm(k), tm(v), tm(alpha), tm(beta)))
            y = tm(outs)
            y = y * jax.lax.rsqrt(jnp.mean(y * y, axis=-1, keepdims=True) + EPS) * head_norm_w
            y = y.reshape(bsz, seq, H * DV)
            gate = jax.nn.sigmoid(jax.nn.silu(x @ u1_w + u1_b) @ u2_w + u2_b)
            y = x + y @ out_w * gate
            y2 = rmsnorm(y, ff_norm_w)
            y = y + jax.nn.silu(y2 @ ff_w1) * (y2 @ ff_w3) @ ff_w2
            return (y, s_final)
        return _reference_tuple_inner(x, norm_in_w, conv_w, conv_b, q_w, k_w, v_w, out_w, alpha_w, alpha_b, beta_w, beta_b, head_norm_w, u1_w, u1_b, u2_w, u2_b, ff_norm_w, ff_w1, ff_w3, ff_w2)[0]

    def _L1_ffn_ref(x, w_gate, w_up, w_down):
        import jax, jax.numpy as jnp
        import numpy as np
        BLOCK = 16
        _GRID = jnp.array([0.0, 0.5, 1.0, 1.5, 2.0, 3.0, 4.0, 6.0], dtype=jnp.float32)
        _MID = jnp.array([0.25, 0.75, 1.25, 1.75, 2.5, 3.5, 5.0], dtype=jnp.float32)

        def fp4_quant_dequant(x):
            shape = x.shape
            xb = x.reshape(shape[:-1] + (shape[-1] // BLOCK, BLOCK))
            scale = jnp.max(jnp.abs(xb), axis=-1, keepdims=True) / 6.0
            scale = jnp.maximum(scale, jnp.float32(1e-12))
            xn = xb / scale
            idx = jnp.searchsorted(_MID, jnp.abs(xn))
            q = _GRID[idx] * jnp.sign(xn) * scale
            return q.reshape(shape)

        def fp4_linear(x, w):
            xq = fp4_quant_dequant(x)
            wq = fp4_quant_dequant(w)
            return jnp.einsum('bsk,nk->bsn', xq, wq)
        gate = fp4_linear(x, w_gate)
        y = fp4_linear(x, w_up)
        h = jax.nn.silu(gate) * y
        return fp4_linear(h, w_down)
    x = x + _L0_xattn_ref(_layernorm(x, axis=-1), ctx_1024, ctx_1024, L0_xattn_Wq, L0_xattn_bq, L0_xattn_Wk, L0_xattn_bk, L0_xattn_Wv, L0_xattn_bv, L0_xattn_Wo, L0_xattn_bo, L0_xattn_rel_k, L0_xattn_rel_v)
    x = x + _L0_attn_ref(_layernorm(x, axis=-1), L0_attn_W_q, L0_attn_W_dkv, L0_attn_W_uk, L0_attn_W_uv, L0_attn_W_o, L0_attn_ln_gamma, L0_attn_ln_beta)
    x = x + _L0_ffn_ref(_layernorm(x, axis=-1), L0_ffn_router_w, L0_ffn_router_b, L0_ffn_w_up, L0_ffn_w_down, L0_ffn_shared_w_up, L0_ffn_shared_w_down)
    x = x + _L1_xattn_ref(_layernorm(x, axis=-1), ctx_1024, mask_BxS2_bf0, L1_xattn_Wq, L1_xattn_bq, L1_xattn_Wkv, L1_xattn_bkv, L1_xattn_Wout, L1_xattn_bout, 16)
    x = x + _L1_attn_ref(_layernorm(x, axis=-1), L1_attn_norm_in_w, L1_attn_conv_w, L1_attn_conv_b, L1_attn_q_w, L1_attn_k_w, L1_attn_v_w, L1_attn_out_w, L1_attn_alpha_w, L1_attn_alpha_b, L1_attn_beta_w, L1_attn_beta_b, L1_attn_head_norm_w, L1_attn_u1_w, L1_attn_u1_b, L1_attn_u2_w, L1_attn_u2_b, L1_attn_ff_norm_w, L1_attn_ff_w1, L1_attn_ff_w3, L1_attn_ff_w2)
    x = x + _L1_ffn_ref(_layernorm(x, axis=-1), L1_ffn_w_gate, L1_ffn_w_up, L1_ffn_w_down)
    return x

_drawn_inputs = setup_inputs


def setup_inputs(seed=0):
    import zlib

    import numpy as np

    out = dict(_drawn_inputs(seed))
    spreads = {'L0_xattn_bq': (0.0, 0.1),
     'L0_xattn_bk': (0.0, 0.8),
     'L0_xattn_bv': (0.0, 0.1),
     'L0_xattn_bo': (0.0, 0.1),
     'L0_attn_ln_gamma': (1.0, 0.2),
     'L0_attn_ln_beta': (0.0, 0.1),
     'L0_ffn_router_b': (0.0, 0.1),
     'L1_xattn_bq': (0.0, 0.56),
     'L1_xattn_bkv': (0.0, 0.1),
     'L1_xattn_bout': (0.0, 0.1),
     'L1_attn_norm_in_w': (1.0, 0.6),
     'L1_attn_conv_b': (0.0, 0.1),
     'L1_attn_alpha_b': (0.0, 0.8),
     'L1_attn_beta_b': (0.0, 0.8),
     'L1_attn_head_norm_w': (1.0, 0.6),
     'L1_attn_u1_b': (0.0, 0.8),
     'L1_attn_u2_b': (0.0, 0.8),
     'L1_attn_ff_norm_w': (1.0, 0.6)}
    factors = {'L0_xattn_rel_k': 8.0,
     'L1_attn_alpha_w': 8.0,
     'L1_attn_beta_w': 8.0,
     'L1_attn_u1_w': 8.0,
     'L1_attn_u2_w': 8.0,
     'L1_attn_ff_w1': 3.938,
     'L1_attn_ff_w3': 3.868,
     'L1_attn_ff_w2': 3.869,
     'L1_ffn_w_gate': 4.663,
     'L1_ffn_w_up': 4.296,
     'L1_ffn_w_down': 4.297}
    for name, (base, spread) in spreads.items():
        noise = np.random.default_rng([zlib.crc32(name.encode()), seed]).standard_normal(out[name].shape)
        drawn = base * np.exp(spread * noise) if base else spread * noise
        out[name] = jnp.asarray(drawn.astype(out[name].dtype))
    for name, factor in factors.items():
        out[name] = (out[name] * factor).astype(out[name].dtype)
    return out
```

```python
import numpy as np
import concourse.bass as bass
from concourse import mybir
from contextlib import ExitStack

F32 = mybir.dt.float32
BF16 = mybir.dt.bfloat16
U8 = mybir.dt.uint8
ALU = mybir.AluOpType
ACT = mybir.ActivationFunctionType
AXX = mybir.AxisListType.X

B, S, D = 16, 64, 256
S2 = 1601
H, HD = 16, 16
NT = B * S // 128
KC = D // 128
NCH = -(-S2 // 128)
CHK = [min(128, S2 - 128 * c) for c in range(NCH)]
NKB = -(-S2 // 512)
KBS = [min(512, S2 - 512 * n) for n in range(NKB)]
GH = [6, 6, 4]
GC = [0, 6 * S, 12 * S]
GR = 96
NEG = -1.0e30
E_MOE, F_MOE = 9, 512
RD = 4


class Bank:

    def __init__(self, base=(0, 0), stride=(0, 0), step=0):
        self.base, self.stride, self.step = base, stride, step
        self.n, self.local = 0, [0, 0]

    def use(self):
        bank = self.n % 2
        self.n += 1
        self.local[bank] += 1
        return bank, self.local[bank]

    def value(self, bank, local):
        return self.base[bank] + self.stride[bank] * self.step + local


class Persistent:

    def __init__(self, nc, ctx, c):
        def sb(name, shape, dt=F32):
            return ctx.enter_context(nc.sbuf_tensor(name, shape, dt))

        self.c = c
        self.X = sb("X", [128, NT, D])
        self.XN = sb("XN", [128, NT, D])
        self.XNT = sb("XNT", [128, KC, NT * 128])
        self.ident = sb("ident", [128, 128])
        self.stats = sb("ln_stats", [128, NT, 6])
        self.mv = sb("ln_mv", [128, NT, 2])
        self.sd = sb("ln_sd", [128, NT])
        self.rs = sb("ln_rs", [128, NT])
        self.PS = ctx.enter_context(nc.psum_tensor("banks", [128, 8, 512], F32))
        self.P = [self.PS[:, i, :] for i in range(8)]
        self.sems = {}
        for n in ("x_in", "bn", "ve", "sd", "rs", "xn", "tr", "xnt"):
            self.sems[n] = ctx.enter_context(nc.semaphore("ln_" + n))



def ln_vector(dve, g, n):
    s = g.sems
    for t in range(NT):
        dve.bn_stats(g.stats[:, t, :], g.X[:, t, :]).then_inc(s["bn"], 1)
    for t in range(NT):
        dve.wait_ge(s["bn"], 2 * NT * n + NT)
        dve.bn_aggr(g.mv[:, t, :], g.stats[:, t, :]).then_inc(s["bn"], 1)
    dve.wait_ge(s["bn"], 2 * NT * (n + 1))
    dve.tensor_scalar(g.rs[:, :], g.mv[:, :, 1], 1e-5, None, ALU.add).then_inc(s["ve"], 1)
    dve.wait_ge(s["sd"], n + 1)
    dve.reciprocal(g.rs[:, :], g.sd[:, :]).then_inc(s["rs"], 1)
    dve.wait_ge(s["rs"], n + 1)
    for t in range(NT):
        dve.tensor_scalar(g.XN[:, t, :], g.X[:, t, :], g.mv[:, t, 0:1], g.rs[:, t:t + 1],
                          ALU.subtract, ALU.mult).then_inc(s["xn"], 1)


def ln_scalar(act, g, n):
    s = g.sems
    act.wait_ge(s["ve"], n + 1)
    act.activation(g.sd[:, :], g.rs[:, :], ACT.Sqrt).then_inc(s["sd"], 1)
    for k in range(NT // 2):
        act.wait_ge(s["tr"], NT // 2 * n + k + 1)
        act.activation(g.XNT[:, :, 256 * k:256 * k + 256],
                       g.P[k][:, :].rearrange("p (c n) -> p c n", c=KC), ACT.Copy).then_inc(s["xnt"], 1)


def ln_tensor(pe, g, n):
    s = g.sems
    for k in range(NT // 2):
        pe.wait_ge(s["xn"], NT * n + 2 * k + 2)
        for c in range(KC):
            for t in (2 * k, 2 * k + 1):
                last = pe.transpose(g.P[k][:, 256 * c + 128 * (t % 2):256 * c + 128 * (t % 2) + 128],
                                    g.XN[:, t, 128 * c:128 * c + 128], g.ident[:, :])
        last.then_inc(s["tr"], 1)


def xnt_ready(eng, g, n):
    eng.wait_ge(g.sems["xnt"], NT // 2 * (n + 1))


def load_x(nc, g, x):
    with nc.Block() as block:
        @block.sync
        def _(sp):
            sp.dma_start(g.X[:, :, :], x).then_inc(g.sems["x_in"], 16)
            sp.dma_start(g.ident[:, :], g.c["ident"]).then_inc(g.sems["x_in"], 16)
            sp.wait_ge(g.sems["x_in"], 32)


def store_x(nc, g, out):
    with nc.Block() as block:
        @block.sync
        def _(sp):
            sp.dma_start(out, g.X[:, :, :]).then_inc(g.sems["x_in"], 16)
            sp.wait_ge(g.sems["x_in"], 48)



def cross_attention(nc, g, n, ctx_t, w, rel=None, mask=None):
    tag = f"x{n}_"
    KR = GR + 1
    with nc.cleanup_on_exit(), ExitStack() as ctx:
        def sb(name, shape, dt=F32):
            return ctx.enter_context(nc.sbuf_tensor(tag + name, shape, dt))

        def sem(name):
            return nc.alloc_semaphore(tag + name)

        wq = sb("wq", [128, KC, 3, GR])
        wk = sb("wk", [128, KC, 3, GR])
        wv = sb("wv", [128, KC, D])
        wo = sb("wo", [128, 4, D])
        bq = sb("bq", [GR, 3])
        bk = sb("bk", [GR, 3])
        bv = sb("bv", [128, 4])
        bo = sb("bo", [128, D])
        hmask = sb("hmask", [GR, 6])
        selden = sb("selden", [128, 128])
        qT = sb("qT", [GR, 3, B * S])
        qs = sb("qs", [GR, 3, S])
        qbd = sb("qbd", [KR, 2, H * S])
        qbf = sb("qbf", [KR, H * S], BF16)
        cT = sb("cT", [128, 2, KC, S2])
        kT = sb("kT", [KR, 2, 3, S2])
        kbf = sb("kbf", [KR, 3, S2], BF16)
        V = sb("V", [128, 2, H, 32])
        PT = sb("PT", [128, 3, H * S])
        one = sb("one", [128, 1])
        mx = sb("mx", [128, H // 2, NKB])
        nm = sb("nm", [128, H // 2])
        oT = sb("oT", [128, 4, S])
        rec = sb("rec", [128, 4 * S])
        oN = sb("oN", [128, 4, S])
        NLOAD = 16 if rel else 12
        if rel:
            relk = sb("relk", [GR, RD + 1])
            rdk = sb("rdk", [GR, RD])
            Rd = sb("Rd", [GR, RD, 6])
            relv = sb("relv", [128, RD + 1, 32])
            rdv = sb("rdv", [128, RD, 32])
            rv4 = sb("rv4", [128, 1])
            rmask = sb("rmask", [128, 2, 128])
            rmaskb = sb("rmaskb", [128, 2, 128], BF16)
            kmask = sb("kmask", [128, RD, S])
            idq = sb("idq", [128, S])
            Ds = sb("Ds", [128, 2, H])
            Dx = sb("Dx", [128, 2, 2, H * S])
            Dxb = sb("Dxb", [128, 2, H * S], BF16)
            Ej = sb("Ej", [128, RD, H * S])
        if mask:
            mT8 = sb("mT8", [128, B * NCH], U8)
            kbias = sb("kbias", [128, B, NCH])
            kbs = sb("kbs", [128, 2, NCH])
            mrow8 = sb("mrow8", [KR, B * S2], U8)

        w_in, ctx_in = sem("w_in"), [[sem(f"ctx_in{p}{k}") for k in range(NKB)] for p in range(2)]
        set_v, set_p, zero_p = sem("set_v"), sem("set_p"), sem("zero_p")
        full = [sem("proj_full0"), sem("proj_full1")]
        free = [sem("proj_free0"), sem("proj_free1")]
        q_full, q_out = sem("q_full"), sem("q_out")
        qs_done, qbd_done, qbf_done = sem("qs_done"), sem("qbd_done"), sem("qbf_done")
        dx_done, dxb_done, kbf_done = sem("dx_done"), sem("dxb_done"), sem("kbf_done")
        max_full, max_read, nm_done = sem("max_full"), sem("max_read"), sem("nm_done")
        s_full, exp_done, av_done = sem("s_full"), sem("exp_done"), sem("av_done")
        kbm_done, tab_done, kbs_done, e_done, rv_done = sem("kbm_done"), sem("tab_done"), sem("kbs_done"), sem("e_done"), sem("rv_done")
        ot_out, mul_done, on_done = sem("ot_out"), sem("mul_done"), sem("on_done")

        PJ, SC, OT, MX = g.P[0:2], g.P[2:5], g.P[5], g.P[6:8]
        UN = 8 * NKB
        SN = 3 * NCH
        NSET = 7 if rel else 3

        class Schedule:

            def __init__(self, bank, ahead, attend, tail):
                self.D = bank.use() if rel and ahead else None
                self.K = [[bank.use() for _ in range(3)] for _ in range(NKB)] if ahead else None
                self.NM = [bank.use() for _ in range(2)] if attend else None
                self.V = []
                for c in range(NCH) if attend else ():
                    self.V.append(bank.use())
                    if tail and c == 2:
                        self.DEN = bank.use()
                    if tail and c == 5:
                        self.WO = bank.use()
                if tail and not attend:
                    self.DEN, self.WO = bank.use(), bank.use()

        SECT, used = [], [0, 0]
        for kinds, steps in (([(True, False, False)], 1),
                             ([(True, True, False), (True, True, True)], 1),
                             ([(True, True, True), (True, True, True)], B // 2 - 2),
                             ([(True, True, True), (False, True, True)], 1),
                             ([(False, False, True)], 1)):
            count = Bank()
            SECT.append((kinds, [Schedule(count, *k) for k in kinds], tuple(used), tuple(count.local)))
            used = [u + steps * x for u, x in zip(used, count.local)]

        def run(eng, body):
            kinds, plans, base, _ = SECT[0]
            body(Bank(base), plans[0], -1, 1, kinds[0])
            kinds, plans, base, _ = SECT[1]
            for p in (0, 1):
                body(Bank(base), plans[p], 0, p, kinds[p])
            kinds, plans, base, stride = SECT[2]
            with eng.Fori(0, B // 2 - 2) as i:
                for p in (0, 1):
                    body(Bank(base, stride, i), plans[p], i + 1, p, kinds[p])
            kinds, plans, base, _ = SECT[3]
            for p in (0, 1):
                body(Bank(base), plans[p], B // 2 - 1, p, kinds[p])
            kinds, plans, base, _ = SECT[4]
            body(Bank(base), plans[0], B // 2, 0, kinds[0])

        def units(c):
            return [(u, u % 8, u // 8) for u in range(UN * c // NCH, UN * (c + 1) // NCH)]

        def later(b, k=1):
            return not (isinstance(b, int) and b < k)

        block = ctx.enter_context(nc.Block())

        @block.sync
        def _(sp):
            loads = [(wq[:, :, :, :], w["wq"]), (wk[:, :, :, :], w["wk"]), (wv[:, :, :], w["wv"]),
                     (wo[:, :, :], w["wo"]), (bq[:, :], w["bq"]), (bk[:, :], w["bk"]), (bv[:, :], w["bv"]),
                     (bo[:, :], w["bo"]), (hmask[:, :], g.c["hmask"]), (selden[:, :], g.c["selden"])]
            if rel:
                loads += [(relk[:, :], rel["k"]), (relv[:, :, :], rel["v"]), (rv4[:, :], rel["v4"]),
                          (rmask[:, :, :], g.c["rmask"]), (kmask[:, :, :], g.c["kmask"]), (idq[:, :], g.c["idq"])]
            if mask:
                loads += [(mT8[:, :], mask["T"]), (mrow8[GR:KR, :], mask["row"])]
            assert len(loads) == NLOAD
            for dst, src in loads:
                sp.dma_start(dst, src).then_inc(w_in, 16)
            for p in (0, 1):
                for k in range(NKB):
                    sp.dma_start(cT[:, p, :, 512 * k:512 * k + KBS[k]],
                                 ctx_t[p, :, :, 512 * k:512 * k + KBS[k]]).then_inc(ctx_in[p][k], 16)
            with sp.Fori(0, B // 2 - 1) as i:
                for p in (0, 1):
                    for k in range(NKB):
                        sp.wait_ge(s_full, (2 * i + p) * SN + 3 * (min(4 * k + 4, NCH) - 1) + 1)
                        sp.dma_start(cT[:, p, :, 512 * k:512 * k + KBS[k]],
                                     ctx_t[bass.ds(2 * i + p + 2, 1), :, :, 512 * k:512 * k + KBS[k]]
                                     .rearrange("a p c n -> p (a c) n")).then_inc(ctx_in[p][k], 16)

        @block.gpsimd
        def _(pool):
            pool.memset(V[:, :, :, :], 0.0).then_inc(zero_p, 1)
            pool.wait_ge(zero_p, 1)
            pool.memset(V[:, :, :, 16:17], 1.0).then_inc(set_p, 1)
            pool.memset(one[:, :], 1.0).then_inc(set_p, 1)

            def body(bank, plan, i, p, flags):
                ahead, attend, tail = flags
                b = 2 * i + p
                if ahead:
                    if attend:
                        pool.wait_ge(max_full, UN * (b + 1))
                    if rel:
                        pb, use = plan.D
                        pool.wait_ge(free[pb], bank.value(pb, use))
                        if later(b):
                            pool.wait_ge(s_full, SN * (b - 1) + 3)
                        for jj in (0, 1):
                            for dst, done in ((Dx[:, 1 - p, jj, :], dx_done), (Dxb[:, jj, :], dxb_done)):
                                pool.tensor_tensor(
                                    dst.rearrange("p (h q) -> p h q", h=H),
                                    Ds[:, jj, :, None].to_broadcast([128, H, S]),
                                    idq[:, None, :].to_broadcast([128, H, S]), ALU.mult).then_inc(done, 1)
                    for k in range(NKB):
                        for gg in (1, 2):
                            pb, use = plan.K[k][gg]
                            pool.wait_ge(free[pb], bank.value(pb, use))
                        pool.tensor_tensor(kbf[0:GR, :, 512 * k:512 * k + KBS[k]],
                                           kT[0:GR, 1 - p, :, 512 * k:512 * k + KBS[k]],
                                           one[0:GR, :, None].to_broadcast([GR, 3, KBS[k]]), ALU.mult).then_inc(kbf_done, 1)
                if attend and rel:
                    pool.wait_ge(exp_done, SN * b + 3)
                    if later(b):
                        pool.wait_ge(rv_done, b)
                    for j in range(RD):
                        pool.tensor_tensor(
                            Ej[:, j, :].rearrange("p (h q) -> p h q", h=H),
                            PT[:, 2, :].rearrange("p (h q) -> p h q", h=H),
                            kmask[:, j, None, :].to_broadcast([128, H, S]), ALU.mult).then_inc(e_done, 1)

            pool.wait_ge(set_p, 2)
            pool.wait_ge(w_in, 16 * NLOAD)
            run(pool, body)

        @block.scalar
        def _(act):
            ln_scalar(act, g, n)
            act.wait_ge(w_in, 16 * NLOAD)
            for u in range(6):
                t, gg = divmod(u, 3)
                act.wait_ge(q_full, u + 1)
                act.activation(qT[:, gg, 512 * t:512 * t + 512], g.P[u][0:GR, :], ACT.Identity,
                               bias=bq[:, gg:gg + 1]).then_inc(q_out, 1)

            def body(bank, plan, i, p, flags):
                ahead, attend, tail = flags
                b = 2 * i + p
                if ahead:
                    if later(b):
                        act.wait_ge(s_full, SN * b)
                        act.wait_ge(kbf_done, NKB * b)
                    for k in range(NKB):
                        for gg in range(3):
                            pb, use = plan.K[k][gg]
                            act.wait_ge(full[pb], bank.value(pb, use))
                            act.activation(kT[0:GR, 1 - p, gg, 512 * k:512 * k + KBS[k]], PJ[pb][0:GR, 0:KBS[k]],
                                           ACT.Identity, bias=bk[:, gg:gg + 1]).then_inc(free[pb], 1)
                if attend:
                    for t in (0, 1):
                        pb, use = plan.NM[t]
                        act.wait_ge(full[pb], bank.value(pb, use))
                        act.activation(qbd[GR:KR, p, 512 * t:512 * t + 512], PJ[pb][GR:KR, :], ACT.Copy)\
                           .then_inc(free[pb], 1)
                    if mask:
                        act.wait_ge(kbs_done, b + 1)
                    for c in range(NCH):
                        slot = 2 if c == 0 else c % 2
                        if c == 0:
                            if later(b):
                                act.wait_ge(av_done, NCH * b)
                                if rel:
                                    act.wait_ge(e_done, RD * b)
                        elif c >= 3:
                            act.wait_ge(av_done, NCH * b + c - 1)
                        for gg in range(3):
                            act.wait_ge(s_full, SN * b + 3 * c + gg + 1)
                            cols = slice(GC[gg], GC[gg] + GH[gg] * S)
                            bias = kbs[0:CHK[c], p, c:c + 1] if mask else 0.0
                            act.activation(PT[0:CHK[c], slot, cols], SC[gg][0:CHK[c], 0:GH[gg] * S], ACT.Exp,
                                           scale=HD ** -0.5, bias=bias).then_inc(exp_done, 1)
                    if rel:
                        act.wait_ge(rv_done, b + 1)
                    else:
                        act.wait_ge(av_done, NCH * (b + 1))
                    if later(b):
                        act.wait_ge(mul_done, b)
                    act.activation(oT[:, :, :], OT[:, 0:4 * S].rearrange("p (j q) -> p j q", j=4), ACT.Copy)\
                       .then_inc(ot_out, 1)

            run(act, body)

        @block.vector
        def _(dve):
            ln_vector(dve, g, n)
            dve.wait_ge(w_in, 16 * NLOAD)
            dve.memset(kT[GR:KR, :, :, :], 1.0).then_inc(set_v, 1)
            dve.memset(qbf[GR:KR, :], NEG).then_inc(set_v, 1)
            dve.wait_ge(g.sems["xn"], NT * (n + 1))
            dve.tensor_tensor(g.X[:, :, :], g.X[:, :, :], bo[:, None, :].to_broadcast([128, NT, D]), ALU.add)\
               .then_inc(set_v, 1)
            if rel:
                dve.tensor_scalar(bv[:, :], bv[:, :], rv4[:, :], None, ALU.add).then_inc(set_v, 1)
                dve.tensor_copy(rmaskb[:, :, :], rmask[:, :, :]).then_inc(set_v, 1)
                dve.tensor_tensor(rdk[:, :], relk[:, 0:RD], relk[:, RD:RD + 1].to_broadcast([GR, RD]), ALU.subtract)\
                   .then_inc(tab_done, 1)
                dve.tensor_tensor(rdv[:, :, :], relv[:, 0:RD, :], relv[:, RD:RD + 1, :].to_broadcast([128, RD, 32]),
                                  ALU.subtract).then_inc(set_v, 1)
                dve.wait_ge(tab_done, 1)
                dve.tensor_tensor(Rd[:, :, :], rdk[:, :, None].to_broadcast([GR, RD, 6]),
                                  hmask[:, None, :].to_broadcast([GR, RD, 6]), ALU.mult).then_inc(set_v, 1)
            else:
                dve.tensor_scalar(kbias[:, :, :], mT8[:, :].rearrange("p (b c) -> p b c", b=B), NEG, None, ALU.mult)\
                   .then_inc(tab_done, 1)
                dve.wait_ge(tab_done, 1)
            dve.wait_ge(q_out, 6)

            def body(bank, plan, i, p, flags):
                ahead, attend, tail = flags
                b = 2 * i + p
                if ahead:
                    if later(b):
                        dve.wait_ge(s_full, SN * b)
                    if attend:
                        dve.wait_ge(qbf_done, b + 1)
                    if mask:
                        if later(b):
                            dve.wait_ge(exp_done, SN * b)
                        dve.tensor_copy(kbs[:, 1 - p:2 - p, :], kbias[:, bass.ds(b + 1, 1), :]).then_inc(kbs_done, 1)
                        if attend:
                            dve.wait_ge(max_full, UN * (b + 1))
                        dve.tensor_copy(kbf[GR:KR, :, :], mrow8[GR:KR, None, bass.ds(S2 * (b + 1), S2)]
                                        .to_broadcast([1, 3, S2])).then_inc(kbm_done, 1)
                    dve.tensor_copy(qs[:, :, :], qT[:, :, bass.ds(S * (b + 1), S)]).then_inc(qs_done, 1)
                    dve.wait_ge(qs_done, b + 2)
                    for gg in range(3):
                        nh = GH[gg]
                        dve.tensor_tensor(
                            qbd[0:GR, 1 - p, GC[gg]:GC[gg] + nh * S].rearrange("p (h q) -> p h q", h=nh),
                            qs[:, gg, None, :].to_broadcast([GR, nh, S]),
                            hmask[:, 0:nh, None].to_broadcast([GR, nh, S]), ALU.mult).then_inc(qbd_done, 1)
                    dve.wait_ge(qbd_done, 3 * (b + 2))
                    dve.tensor_copy(qbf[0:GR, :], qbd[0:GR, 1 - p, :]).then_inc(qbf_done, 1)
                    if rel:
                        pb, use = plan.D
                        dve.wait_ge(full[pb], bank.value(pb, use))
                        if attend:
                            dve.wait_ge(dxb_done, 2 * (b + 1))
                        dve.tensor_copy(Ds[:, :, :], PJ[pb][:, 0:2 * H].rearrange("p (j h) -> p j h", j=2))\
                           .then_inc(free[pb], 1)

                def denominators():
                    pb, use = plan.DEN
                    dve.wait_ge(full[pb], bank.value(pb, use))
                    dve.reciprocal(rec[:, :], PJ[pb][:, 0:4 * S]).then_inc(free[pb], 1)
                    dve.wait_ge(free[pb], bank.value(pb, use))
                    dve.tensor_tensor(oN[:, :, :], oT[:, :, :], rec[:, :].rearrange("p (j q) -> p j q", j=4), ALU.mult)\
                       .then_inc(mul_done, 1)
                    dve.wait_ge(mul_done, b)
                    dve.tensor_tensor(oN[:, :, :], oN[:, :, :], bv[:, :, None].to_broadcast([128, 4, S]), ALU.add)\
                       .then_inc(on_done, 1)

                def add_output():
                    pb, use = plan.WO
                    dve.wait_ge(full[pb], bank.value(pb, use))
                    tile = i if p else i - 1
                    x = g.X[64 * (1 - p):64 * (1 - p) + 64, bass.ds(tile, 1), :]
                    dve.tensor_tensor(x, x, PJ[pb][64 * (1 - p):64 * (1 - p) + 64, None, 0:D], ALU.add)\
                       .then_inc(free[pb], 1)

                def maxima(us):
                    for u, hp, kb in us:
                        dve.wait_ge(max_full, UN * (b + 1) + u + 1)
                        dve.reduce_max(mx[:, hp, kb:kb + 1], MX[u % 2][:, 0:KBS[kb]], AXX).then_inc(max_read, 1)

                for c in range(NCH) if attend else ():
                    pb, use = plan.V[c]
                    dve.wait_ge(full[pb], bank.value(pb, use))
                    if later(b) or c >= 2:
                        dve.wait_ge(av_done, NCH * b + (c - 1 if c >= 2 else 0))
                    dve.tensor_copy(V[0:CHK[c], c % 2, :, 0:HD],
                                    PJ[pb][0:CHK[c], 0:D].rearrange("p (h d) -> p h d", h=H)).then_inc(free[pb], 1)
                    if ahead:
                        maxima(units(c))
                    if tail and c == 2:
                        denominators()
                    if tail and c == 5:
                        add_output()
                if ahead:
                    if not attend:
                        maxima([(u, u % 8, u // 8) for u in range(UN)])
                    dve.wait_ge(max_read, UN * (b + 2))
                    dve.tensor_reduce(nm[:, :], mx[:, :, :], AXX, ALU.max, negate=True).then_inc(nm_done, 1)
                if tail and not attend:
                    denominators()
                    add_output()

            run(dve, body)

        @block.tensor
        def _(pe):
            ln_tensor(pe, g, n)
            pe.wait_ge(w_in, 16 * NLOAD)
            xnt_ready(pe, g, n)
            for u in range(6):
                t, gg = divmod(u, 3)
                for c in range(KC):
                    last = pe.matmul(g.P[u][0:GR, :], wq[:, c, gg, :], g.XNT[:, c, 512 * t:512 * t + 512],
                                     start=c == 0, stop=c == KC - 1)
                last.then_inc(q_full, 1)
            pe.wait_ge(set_v, NSET)
            pe.wait_ge(set_p, 2)
            pe.wait_ge(q_out, 6)

            def body(bank, plan, i, p, flags):
                ahead, attend, tail = flags
                b = 2 * i + p

                def take(where):
                    pb, use = where
                    if not (isinstance(bank.value(pb, use), int) and bank.value(pb, use) <= 1):
                        pe.wait_ge(free[pb], bank.value(pb, use) - 1)
                    return pb

                def context_in(k, ahead):
                    q = (p + ahead) % 2
                    pe.wait_ge(ctx_in[q][k], 16 * (i + 1 + (p + ahead) // 2))

                def maxima(us):
                    for u, hp, kb in us:
                        if u == 0:
                            pe.wait_ge(qbf_done, b + 2)
                            if rel:
                                pe.wait_ge(dxb_done, 2 * (b + 2))
                            if mask:
                                pe.wait_ge(kbm_done, b + 2)
                        if u % 8 == 0:
                            pe.wait_ge(kbf_done, NKB * (b + 1) + kb + 1)
                        if u >= 2 or attend:
                            pe.wait_ge(max_read, UN * (b + 1) + u - 1)
                        rows = KR if mask else GR
                        out = MX[u % 2]
                        gg = 0 if hp < 3 else 1 if hp < 6 else 2
                        more = rel and kb == 0
                        last = pe.matmul(out[:, 0:KBS[kb]], qbf[0:rows, 128 * hp:128 * hp + 128],
                                         kbf[0:rows, gg, 512 * kb:512 * kb + KBS[kb]], start=True, stop=not more)
                        for jj in (0, 1) if more else ():
                            last = pe.matmul(out[:, 0:128], Dxb[:, jj, 128 * hp:128 * hp + 128], rmaskb[:, jj, :],
                                             start=False, stop=jj == 1)
                        last.then_inc(max_full, 1)

                def denominators():
                    pb = take(plan.DEN)
                    pe.wait_ge(ot_out, b)
                    pe.matmul(PJ[pb][:, 0:4 * S], selden[:, :], oT[:, :, :].rearrange("p j q -> p (j q)"),
                              start=True, stop=True).then_inc(full[pb], 1)

                def output():
                    pb = take(plan.WO)
                    pe.wait_ge(on_done, b)
                    for j in range(4):
                        last = pe.matmul(PJ[pb][64 * (1 - p):64 * (1 - p) + 64, 0:D], oN[:, j, :], wo[:, j, :],
                                         start=j == 0, stop=j == 3)
                    last.then_inc(full[pb], 1)

                def attend_values(c):
                    pe.wait_ge(exp_done, SN * b + 3 * c + 3)
                    pb, use = plan.V[c]
                    pe.wait_ge(free[pb], bank.value(pb, use))
                    if c == 0 and later(b):
                        pe.wait_ge(ot_out, b)
                    slot = 2 if c == 0 else c % 2
                    for h in range(H):
                        r = 32 * (h % 4)
                        last = pe.matmul(OT[r:r + 32, S * (h // 4):S * (h // 4) + S], V[0:CHK[c], c % 2, h, :],
                                         PT[0:CHK[c], slot, S * h:S * h + S], start=c == 0 and h < 4,
                                         stop=c == NCH - 1 and not rel, skip_group_check=True)
                    last.then_inc(av_done, 1)

                if ahead:
                    if rel:
                        pb = take(plan.D)
                        pe.wait_ge(qs_done, b + 2)
                        for jp in (0, 1):
                            for gg in range(3):
                                out = PJ[pb][64 * jp:64 * jp + 64, 0:2 * H].rearrange("p (j h) -> p j h", j=2)
                                last = pe.matmul(out[:, :, 6 * gg:6 * gg + GH[gg]], qs[:, gg, :],
                                                 Rd[:, jp:RD:2, 0:GH[gg]], start=True, stop=True)
                        last.then_inc(full[pb], 1)
                    for k in range(NKB):
                        context_in(k, 1)
                        for gg in range(3):
                            pb = take(plan.K[k][gg])
                            for c in range(KC):
                                last = pe.matmul(PJ[pb][0:GR, 0:KBS[k]], wk[:, c, gg, :],
                                                 cT[:, (p + 1) % 2, c, 512 * k:512 * k + KBS[k]],
                                                 start=c == 0, stop=c == KC - 1)
                            last.then_inc(full[pb], 1)
                if attend:
                    pe.wait_ge(nm_done, b + 1)
                    for t in (0, 1):
                        pb = take(plan.NM[t])
                        for k in range(4):
                            last = pe.matmul(PJ[pb][GR:GR + 1, 128 * k:128 * k + 128], nm[:, 4 * t + k:4 * t + k + 1],
                                             g.ident[:, :], start=True, stop=True)
                        last.then_inc(full[pb], 1)
                    for c in range(NCH):
                        pb = take(plan.V[c])
                        for cc in range(KC):
                            last = pe.matmul(PJ[pb][0:CHK[c], 0:D], cT[:, p, cc, 128 * c:128 * c + CHK[c]],
                                             wv[:, cc, :], start=cc == 0, stop=cc == KC - 1)
                        last.then_inc(full[pb], 1)
                        if c == 0:
                            for where in plan.NM:
                                pe.wait_ge(free[where[0]], bank.value(*where))
                        for gg in range(3):
                            if c or later(b):
                                pe.wait_ge(exp_done, SN * b + 3 * c + gg - 2)
                            more = rel and c == 0
                            cols = slice(GC[gg], GC[gg] + GH[gg] * S)
                            out = SC[gg][0:CHK[c], 0:GH[gg] * S]
                            last = pe.matmul(out, kT[:, p, gg, 128 * c:128 * c + CHK[c]], qbd[:, p, cols],
                                             start=True, stop=not more)
                            for jj in (0, 1) if more else ():
                                last = pe.matmul(out, rmask[:, jj, :], Dx[:, p, jj, cols], start=False, stop=jj == 1)
                            last.then_inc(s_full, 1)
                        if ahead:
                            maxima(units(c))
                        if tail and c == 2:
                            denominators()
                        if tail and c == 5:
                            output()
                        if c:
                            attend_values(c - 1)
                    attend_values(NCH - 1)
                    if rel:
                        pe.wait_ge(e_done, RD * (b + 1))
                        for j in range(RD):
                            for r in range(4):
                                ej = Ej[:, j, :].rearrange("p (k r q) -> p r k q", r=4, q=S)[:, r]
                                last = pe.matmul(OT[32 * r:32 * r + 32, 0:4 * S], rdv[:, j, :], ej,
                                                 start=False, stop=j == RD - 1, skip_group_check=True)
                        last.then_inc(rv_done, 1)
                if ahead and not attend:
                    maxima([(u, u % 8, u // 8) for u in range(UN)])
                if tail and not attend:
                    denominators()
                    output()

            run(pe, body)



LAT = 64
HR = HD // 2


def latent_attention(nc, g, n, w):
    tag = f"l{n}_"
    with nc.cleanup_on_exit(), ExitStack() as ctx:
        def sb(name, shape, dt=F32):
            return ctx.enter_context(nc.sbuf_tensor(tag + name, shape, dt))

        def sem(name):
            return nc.alloc_semaphore(tag + name)

        wq, wd = sb("wq", [128, KC, D]), sb("wd", [128, KC, LAT])
        wuk, wuv = sb("wuk", [LAT, D]), sb("wuv", [LAT, D])
        wo = sb("wo", [128, 2, D])
        bdm = sb("bdm", [128, 2])
        gam, bet = sb("gam", [128, LAT]), sb("bet", [128, LAT])
        cos, sin = sb("cos", [128, HR]), sb("sin", [128, HR])
        hmask = sb("hmask", [128, 8])
        causal = sb("causal", [128, S])
        qn, kn = sb("qn", [128, NT, D]), sb("kn", [128, NT, D])
        qr, kr = sb("qr", [128, NT, D]), sb("kr", [128, NT, D])
        ra, rb = sb("ra", [128, NT * H, HR]), sb("rb", [128, NT * H, HR])
        rc, rd = sb("rc", [128, NT * H, HR]), sb("rd", [128, NT * H, HR])
        qT, kT = sb("qT", [128, KC, B * S]), sb("kT", [128, KC, B * S])
        lat = sb("lat", [128, NT, LAT])
        latT = sb("latT", [LAT, B * S])
        st, mv = sb("st", [128, NT, 6]), sb("mv", [128, NT, 2])
        ve, sd, rs = sb("ve", [128, NT]), sb("sd", [128, NT]), sb("rs", [128, NT])
        vn = sb("vn", [128, B, D])
        qbd = sb("qbd", [128, 2, KC, 8 * S])
        V = sb("V", [128, 2, 8, 32])
        sc = sb("sc", [128, 2, 8, S])
        m, den, rden = sb("m", [128, 8]), sb("den", [128, 8]), sb("rden", [128, 8])
        PT = sb("PT", [128, 4, 2, S])
        oT = sb("oT", [128, 2, S])

        w_in = sem("w_in")
        p_full, q_out, lat_out = sem("p_full"), sem("q_out"), sem("lat_out")
        bn, ve_done, sd_done, rs_done, ln = sem("bn"), sem("ve_done"), sem("sd_done"), sem("rs_done"), sem("ln")
        lt_full, lt_out, k_full, k_out, v_full, vn_out = (
            sem("lt_full"), sem("lt_out"), sem("k_full"), sem("k_out"), sem("v_full"), sem("vn_out"))
        rq, rk = sem("rq"), sem("rk")
        t_full, t_out = sem("t_full"), sem("t_out")
        qbd_done, v_done = sem("qbd_done"), sem("v_done")
        s_full, step, sub_done, ex_done, pn_done = sem("s_full"), sem("step"), sem("sub_done"), sem("ex_done"), sem("pn_done")
        tr_full, pt_out, av_full, ot_out, wo_full, x_done = (
            sem("tr_full"), sem("pt_out"), sem("av_full"), sem("ot_out"), sem("wo_full"), sem("x_done"))
        NL = 12

        def rotate(eng, s, x, out, a, b):
            xv = x[:, :, :].rearrange("p t (h d) -> p (t h) d", d=HD)
            ov = out[:, :, :].rearrange("p t (h d) -> p (t h) d", d=HD)
            cb = cos[:, None, :].to_broadcast([128, NT * H, HR])
            sb_ = sin[:, None, :].to_broadcast([128, NT * H, HR])
            for k, (t1, t2, op) in enumerate(((cb, sb_, ALU.subtract), (sb_, cb, ALU.add))):
                if k:
                    eng.wait_ge(s, 3)
                eng.tensor_tensor(a[:, :, :], xv[:, :, 0:HR], t1, ALU.mult).then_inc(s, 1)
                eng.tensor_tensor(b[:, :, :], xv[:, :, HR:HD], t2, ALU.mult).then_inc(s, 1)
                eng.wait_ge(s, 3 * k + 2)
                eng.tensor_tensor(ov[:, :, HR * k:HR * k + HR], a[:, :, :], b[:, :, :], op).then_inc(s, 1)

        def run(eng, body):
            body(-1, 1, True, False)
            body(0, 0, True, True)
            body(0, 1, True, True)
            with eng.Fori(0, B // 2 - 2) as i:
                for p in (0, 1):
                    body(i + 1, p, True, True)
            body(B // 2 - 1, 0, True, True)
            body(B // 2 - 1, 1, False, True)

        def later(b, k=1):
            return not (isinstance(b, int) and b < k)

        block = ctx.enter_context(nc.Block())

        @block.sync
        def _(sp):
            for dst, src in ((wq[:, :, :], w["W_q"]), (wd[:, :, :], w["W_dkv"]), (wuk[:, :], w["W_uk"]),
                             (wuv[:, :], w["W_uv"]), (wo[:, :, :], w["W_o"]), (gam[:, :], w["gamma"]),
                             (bet[:, :], w["beta"]), (cos[:, :], g.c["cos"]), (sin[:, :], g.c["sin"]),
                             (hmask[:, :], g.c["hmask8"]), (causal[:, :], g.c["causal"]), (bdm[:, :], g.c["bdm"])):
                sp.dma_start(dst, src).then_inc(w_in, 16)

        @block.gpsimd
        def _(pool):
            pool.wait_ge(w_in, 16 * NL)
            pool.wait_ge(q_out, NT)
            rotate(pool, rq, qn, qr, ra, rb)
            pool.wait_ge(t_out, 8)
            pool.wait_ge(vn_out, B // 2)

            def body(i, p, ahead, attend):
                b = 2 * i + p
                if ahead:
                    if later(b):
                        pool.wait_ge(s_full, b)
                    pool.tensor_tensor(
                        qbd[:, 1 - p, :, :].rearrange("p c (h q) -> p c h q", h=8),
                        qT[:, :, None, bass.ds(S * (b + 1), S)].to_broadcast([128, KC, 8, S]),
                        hmask[:, None, :, None].to_broadcast([128, KC, 8, S]), ALU.mult).then_inc(qbd_done, 1)
                    if later(b):
                        pool.wait_ge(av_full, b)
                    pool.tensor_tensor(V[:, 1 - p, :, :].rearrange("p n (o d) -> p n o d", o=2),
                                       vn[:, bass.ds(b + 1, 1), :].rearrange("p a (n o d) -> p (a n) o d", o=2, d=HD),
                                       bdm[:, None, :, None].to_broadcast([128, 8, 2, HD]), ALU.mult).then_inc(v_done, 1)

            run(pool, body)

        @block.scalar
        def _(act):
            ln_scalar(act, g, n)
            act.wait_ge(w_in, 16 * NL)
            for t in range(NT):
                act.wait_ge(p_full, t + 1)
                act.activation(qn[:, t, :], g.P[t][:, 0:D], ACT.Copy).then_inc(q_out, 1)
            act.wait_ge(ve_done, 1)
            act.activation(sd[:, :], ve[:, :], ACT.Sqrt).then_inc(sd_done, 1)
            for k in range(2):
                act.wait_ge(lt_full, k + 1)
                act.activation(latT[:, 512 * k:512 * k + 512], g.P[k][0:LAT, :], ACT.Copy).then_inc(lt_out, 1)
            for t in range(B // 2):
                act.wait_ge(v_full, t + 1)
                act.activation(vn[:, 2 * t:2 * t + 2, :], g.P[4 + t % 4].rearrange("p (b n) -> p b n", b=2),
                               ACT.Copy).then_inc(vn_out, 1)
            for k in range(8):
                act.wait_ge(t_full, k + 1)
                dst = qT if k < 4 else kT
                act.activation(dst[:, :, 256 * (k % 4):256 * (k % 4) + 256],
                               g.P[k][:, :].rearrange("p (c n) -> p c n", c=KC), ACT.Copy).then_inc(t_out, 1)

            def body(i, p, ahead, attend):
                b = 2 * i + p
                if attend:
                    act.wait_ge(tr_full, b + 1)
                    if later(b):
                        act.wait_ge(av_full, b)
                    act.activation(PT[:, :, :, :], g.P[2 + p].rearrange("p (a e q) -> p a e q", a=4, e=2), ACT.Copy)\
                       .then_inc(pt_out, 1)
                if ahead:
                    act.wait_ge(sub_done, b + 2)
                    act.activation(sc[:, 1 - p, :, :], sc[:, 1 - p, :, :], ACT.Exp, scale=HD ** -0.5).then_inc(ex_done, 1)
                if attend:
                    act.wait_ge(av_full, b + 1)
                    if later(b):
                        act.wait_ge(wo_full, b)
                    act.activation(oT[:, :, :], g.P[4][:, 0:2 * S].rearrange("p (j q) -> p j q", j=2), ACT.Copy)\
                       .then_inc(ot_out, 1)

            run(act, body)

        @block.vector
        def _(dve):
            ln_vector(dve, g, n)
            for t in range(NT):
                dve.wait_ge(q_out, t + 1)
                dve.tensor_copy(lat[:, t, :], g.P[t][:, D:D + LAT]).then_inc(lat_out, 1)
            dve.wait_ge(lat_out, NT)
            for t in range(NT):
                dve.bn_stats(st[:, t, :], lat[:, t, :]).then_inc(bn, 1)
            dve.wait_ge(bn, NT)
            for t in range(NT):
                dve.bn_aggr(mv[:, t, :], st[:, t, :]).then_inc(bn, 1)
            dve.wait_ge(bn, 2 * NT)
            dve.tensor_scalar(ve[:, :], mv[:, :, 1], 1e-5, None, ALU.add).then_inc(ve_done, 1)
            dve.wait_ge(sd_done, 1)
            dve.reciprocal(rs[:, :], sd[:, :]).then_inc(rs_done, 1)
            dve.wait_ge(rs_done, 1)
            for t in range(NT):
                dve.tensor_scalar(lat[:, t, :], lat[:, t, :], mv[:, t, 0:1], rs[:, t:t + 1],
                                  ALU.subtract, ALU.mult).then_inc(ln, 1)
            dve.wait_ge(w_in, 16 * NL)
            dve.wait_ge(ln, NT)
            dve.tensor_tensor(lat[:, :, :], lat[:, :, :], gam[:, None, :].to_broadcast([128, NT, LAT]), ALU.mult).then_inc(ln, 1)
            dve.wait_ge(ln, NT + 1)
            dve.tensor_tensor(lat[:, :, :], lat[:, :, :], bet[:, None, :].to_broadcast([128, NT, LAT]), ALU.add).then_inc(ln, 1)
            for k in range(NT // 2):
                dve.wait_ge(k_full, k + 1)
                dve.tensor_copy(kn[:, 2 * k:2 * k + 2, :], g.P[k][:, :].rearrange("p (t n) -> p t n", t=2)).then_inc(k_out, 1)
            dve.wait_ge(k_out, NT // 2)
            rotate(dve, rk, kn, kr, rc, rd)

            def body(i, p, ahead, attend):
                b = 2 * i + p
                if ahead:
                    x = sc[:, 1 - p, :, :]
                    dve.wait_ge(s_full, b + 2)
                    if later(b):
                        dve.wait_ge(tr_full, b)
                    dve.tensor_tensor(x, g.P[1 - p][:, :].rearrange("p (h k) -> p h k", k=S),
                                      causal[:, None, :].to_broadcast([128, 8, S]), ALU.add).then_inc(step, 1)
                    dve.wait_ge(step, 4 * (b + 1) + 1)
                    dve.reduce_max(m[:, :], x, AXX).then_inc(step, 1)
                    dve.wait_ge(step, 4 * (b + 1) + 2)
                    dve.tensor_tensor(x, x, m[:, :, None].to_broadcast([128, 8, S]), ALU.subtract).then_inc(sub_done, 1)
                    dve.wait_ge(ex_done, b + 2)
                    dve.reduce_sum(den[:, :], x, AXX).then_inc(step, 1)
                    dve.wait_ge(step, 4 * (b + 1) + 3)
                    dve.reciprocal(rden[:, :], den[:, :]).then_inc(step, 1)
                    dve.wait_ge(step, 4 * (b + 1) + 4)
                    dve.tensor_tensor(x, x, rden[:, :, None].to_broadcast([128, 8, S]), ALU.mult).then_inc(pn_done, 1)
                if attend:
                    dve.wait_ge(wo_full, b + 1)
                    y = g.X[64 * p:64 * p + 64, bass.ds(i, 1), :]
                    dve.tensor_tensor(y, y, g.P[5 + p][64 * p:64 * p + 64, None, 0:D], ALU.add).then_inc(x_done, 1)

            run(dve, body)

        @block.tensor
        def _(pe):
            ln_tensor(pe, g, n)
            pe.wait_ge(w_in, 16 * NL)
            xnt_ready(pe, g, n)
            for t in range(NT):
                for c in range(KC):
                    pe.matmul(g.P[t][:, 0:D], g.XNT[:, c, 128 * t:128 * t + 128], wq[:, c, :], start=c == 0, stop=c == KC - 1)
                for c in range(KC):
                    last = pe.matmul(g.P[t][:, D:D + LAT], g.XNT[:, c, 128 * t:128 * t + 128], wd[:, c, :],
                                     start=c == 0, stop=c == KC - 1)
                last.then_inc(p_full, 1)
            pe.wait_ge(ln, NT + 2)
            pe.wait_ge(q_out, NT)
            for k in range(2):
                for t in range(4):
                    last = pe.transpose(g.P[k][0:LAT, 128 * t:128 * t + 128], lat[:, 4 * k + t, :], g.ident[:, :])
                last.then_inc(lt_full, 1)
            pe.wait_ge(lt_out, 2)
            for k in range(NT // 2):
                for t in (0, 1):
                    last = pe.matmul(g.P[k][:, D * t:D * t + D], latT[:, 128 * (2 * k + t):128 * (2 * k + t) + 128], wuk[:, :],
                                     start=True, stop=True)
                last.then_inc(k_full, 1)
            for t in range(B // 2):
                if t >= 4:
                    pe.wait_ge(vn_out, t - 3)
                for k in (0, 1):
                    b = 2 * t + k
                    for o in (0, 1):
                        last = pe.matmul(g.P[4 + t % 4][64 * o:64 * o + 64, D * k:D * k + D],
                                         latT[:, S * b:S * b + S], wuv[:, :], start=True, stop=True)
                last.then_inc(v_full, 1)
            for k in range(8):
                src = qr if k < 4 else kr
                if k == 0:
                    pe.wait_ge(rq, 6)
                    pe.wait_ge(k_out, NT // 2)
                if k == 4:
                    pe.wait_ge(rk, 6)
                    pe.wait_ge(vn_out, B // 2)
                for c in range(KC):
                    for t in (0, 1):
                        last = pe.transpose(g.P[k][:, 256 * c + 128 * t:256 * c + 128 * t + 128],
                                            src[:, 2 * (k % 4) + t, 128 * c:128 * c + 128], g.ident[:, :])
                last.then_inc(t_full, 1)
            pe.wait_ge(t_out, 8)

            def body(i, p, ahead, attend):
                b = 2 * i + p
                if ahead:
                    pe.wait_ge(qbd_done, b + 2)
                    if later(b):
                        pe.wait_ge(sub_done, b)
                    for hp in range(8):
                        last = pe.matmul(g.P[1 - p][:, S * hp:S * hp + S], qbd[:, 1 - p, hp // 4, 128 * (hp % 4):128 * (hp % 4) + 128],
                                         kT[:, hp // 4, bass.ds(S * (b + 1), S)], start=True, stop=True)
                    last.then_inc(s_full, 1)
                if attend:
                    pe.wait_ge(pn_done, b + 1)
                    for a in range(4):
                        last = pe.transpose(g.P[2 + p][:, 128 * a:128 * a + 128],
                                            sc[:, p, 2 * a:2 * a + 2, :].rearrange("p h k -> p (h k)"), g.ident[:, :])
                    last.then_inc(tr_full, 1)
                    pe.wait_ge(pt_out, b + 1)
                    pe.wait_ge(v_done, b + 1)
                    if later(b):
                        pe.wait_ge(ot_out, b)
                    for k in range(8):
                        r, j = 32 * (k % 4), k // 4
                        last = pe.matmul(g.P[4][r:r + 32, S * j:S * j + S], V[:, p, k, :], PT[:, k // 2, k % 2, :],
                                         start=True, stop=True)
                    last.then_inc(av_full, 1)
                    pe.wait_ge(ot_out, b + 1)
                    if later(b, 2):
                        pe.wait_ge(x_done, b - 1)
                    for j in range(2):
                        last = pe.matmul(g.P[5 + p][64 * p:64 * p + 64, 0:D], oT[:, j, :], wo[:, j, :], start=j == 0, stop=j == 1)
                    last.then_inc(wo_full, 1)

            run(pe, body)



NR = 8
FC = F_MOE // 128


def moe(nc, g, n, w):
    tag = f"e{n}_"
    with nc.cleanup_on_exit(), ExitStack() as ctx:
        def sb(name, shape, dt=F32):
            return ctx.enter_context(nc.sbuf_tensor(tag + name, shape, dt))

        def sem(name):
            return nc.alloc_semaphore(tag + name)

        wu, wd = sb("wu", [128, 2, KC, F_MOE]), sb("wd", [128, 2, FC, D])
        wr, br = sb("wr", [128, KC, NR]), sb("br", [128, NR])
        tri = sb("tri", [128, NR, NR])
        pr = sb("pr", [128, NT, NR])
        m, den = sb("m", [128, NT]), sb("den", [128, NT])
        gt, eq = sb("gt", [128, NT, NR, NR]), sb("eq", [128, NT, NR, NR])
        rank, picked = sb("rank", [128, NT, NR]), sb("picked", [128, NT, NR])
        comb = sb("comb", [128, NT, E_MOE])
        hT = sb("hT", [128, 2, FC, 512])

        w_in, wu_in, wd_in = sem("w_in"), [sem("wu_in0"), sem("wu_in1")], [sem("wd_in0"), sem("wd_in1")]
        r_full, st, ex_done = sem("r_full"), sem("st"), sem("ex_done")
        up_full, h_out, dn_full, acc = sem("up_full"), sem("h_out"), sem("dn_full"), sem("acc")

        def run(eng, body):
            body(0, 0, True)
            body(0, 1, False)
            with eng.Fori(0, NR // 2 - 1) as i:
                body(i + 1, 0, False)
                body(i + 1, 1, False)
            body(NR // 2, 0, False)

        block = ctx.enter_context(nc.Block())

        @block.sync
        def _(sp):
            for dst, src in ((wr[:, :, :], w["wr"]), (br[:, :], w["br"]), (tri[:, :, :], g.c["tri"])):
                sp.dma_start(dst, src).then_inc(w_in, 16)

            def load(q, e):
                sp.dma_start(wu[:, q, :, :], w["up"][bass.ds(e, 1)].rearrange("a p c n -> p (a c) n")).then_inc(wu_in[q], 16)
                sp.dma_start(wd[:, q, :, :], w["down"][bass.ds(e, 1)].rearrange("a p c n -> p (a c) n")).then_inc(wd_in[q], 16)

            load(0, 0)
            load(1, 1)
            with sp.Fori(0, NR // 2 - 1) as i:
                for q in (0, 1):
                    sp.wait_ge(dn_full, NT * (2 * i + q + 1))
                    load(q, 2 * i + q + 2)
            sp.wait_ge(dn_full, NT * (NR - 1))
            load(0, NR)

        @block.scalar
        def _(act):
            ln_scalar(act, g, n)
            act.wait_ge(st, 2)
            act.activation(pr[:, :, :], pr[:, :, :], ACT.Exp).then_inc(ex_done, 1)

            def body(i, q, first):
                e = 2 * i + q
                for t in (0, 1):
                    for f in range(FC):
                        act.wait_ge(up_full, FC * (2 * e + t) + f + 1)
                        if f == 0 and not first:
                            act.wait_ge(dn_full, 4 * (2 * e + t - 1))
                        act.activation(hT[:, t, f, :], g.P[f][:, :], ACT.Silu).then_inc(h_out, 1)

            run(act, body)

        @block.vector
        def _(dve):
            ln_vector(dve, g, n)
            dve.wait_ge(w_in, 48)
            dve.wait_ge(r_full, 1)
            dve.tensor_tensor(pr[:, :, :], g.P[0][:, 0:NT * NR].rearrange("p (t e) -> p t e", t=NT),
                              br[:, None, :].to_broadcast([128, NT, NR]), ALU.add).then_inc(st, 1)
            dve.wait_ge(st, 1)
            dve.reduce_max(m[:, :], pr[:, :, :], AXX).then_inc(acc, 1)
            dve.wait_ge(acc, 1)
            dve.tensor_tensor(pr[:, :, :], pr[:, :, :], m[:, :, None].to_broadcast([128, NT, NR]), ALU.subtract).then_inc(st, 1)
            k = 2

            def after(ins):
                nonlocal k
                k += 1
                ins.then_inc(st, 1)
                dve.wait_ge(st, k)

            pj = pr[:, :, None, :].to_broadcast([128, NT, NR, NR])
            pe_ = pr[:, :, :, None].to_broadcast([128, NT, NR, NR])
            dve.wait_ge(ex_done, 1)
            after(dve.reduce_sum(den[:, :], pr[:, :, :], AXX))
            after(dve.reciprocal(m[:, :], den[:, :]))
            after(dve.tensor_tensor(pr[:, :, :], pr[:, :, :], m[:, :, None].to_broadcast([128, NT, NR]), ALU.mult))
            after(dve.tensor_tensor(gt[:, :, :, :], pj, pe_, ALU.is_gt))
            after(dve.tensor_tensor(eq[:, :, :, :], pj, pe_, ALU.is_equal))
            after(dve.tensor_tensor(eq[:, :, :, :], eq[:, :, :, :], tri[:, None, :, :].to_broadcast([128, NT, NR, NR]), ALU.mult))
            after(dve.tensor_tensor(gt[:, :, :, :], gt[:, :, :, :], eq[:, :, :, :], ALU.add))
            after(dve.reduce_sum(rank[:, :, :], gt[:, :, :, :], AXX))
            after(dve.scalar_tensor_tensor(picked[:, :, :], rank[:, :, :], 1.5, pr[:, :, :], ALU.is_lt, ALU.mult))
            after(dve.reduce_sum(den[:, :], picked[:, :, :], AXX))
            after(dve.reciprocal(m[:, :], den[:, :]))
            after(dve.tensor_tensor(comb[:, :, 0:NR], picked[:, :, :], m[:, :, None].to_broadcast([128, NT, NR]), ALU.mult))
            after(dve.memset(comb[:, :, NR:E_MOE], 1.0))

            def body(i, q, first):
                e = 2 * i + q
                for t in range(NT):
                    dve.wait_ge(dn_full, NT * e + t + 1)
                    if t == 0:
                        dve.wait_ge(acc, NT * e + 1)
                    dve.scalar_tensor_tensor(g.X[:, t, :], g.P[4 + t % 4][:, 0:D], comb[:, t, bass.ds(e, 1)], g.X[:, t, :],
                                             ALU.mult, ALU.add).then_inc(acc, 1)

            run(dve, body)

        @block.tensor
        def _(pe):
            ln_tensor(pe, g, n)
            pe.wait_ge(w_in, 48)
            xnt_ready(pe, g, n)
            for t in range(NT):
                for c in range(KC):
                    last = pe.matmul(g.P[0][:, NR * t:NR * t + NR], g.XNT[:, c, 128 * t:128 * t + 128], wr[:, c, :],
                                     start=c == 0, stop=c == KC - 1)
            last.then_inc(r_full, 1)
            pe.wait_ge(st, 1)

            def up(i, q, t, first):
                e = 2 * i + q
                if t == 0:
                    pe.wait_ge(wu_in[q], 16 * (i + 1))
                for f in range(FC):
                    if not (first and t == 0):
                        pe.wait_ge(h_out, FC * (2 * e + t - 1) + f + 1)
                    for c in range(KC):
                        last = pe.matmul(g.P[f][:, :], wu[:, q, c, 128 * f:128 * f + 128],
                                         g.XNT[:, c, 512 * t:512 * t + 512], start=c == 0, stop=c == KC - 1)
                    last.then_inc(up_full, 1)

            def down(i, q, t):
                e = 2 * i + q
                if t == 0:
                    pe.wait_ge(wd_in[q], 16 * (i + 1))
                pe.wait_ge(h_out, FC * (2 * e + t + 1))
                for k in range(4):
                    if not (isinstance(e, int) and e == 0 and t == 0):
                        pe.wait_ge(acc, NT * e + 4 * t + k - 3 + 1)
                    for f in range(FC):
                        last = pe.matmul(g.P[4 + k][:, 0:D], hT[:, t, f, 128 * k:128 * k + 128], wd[:, q, f, :],
                                         start=f == 0, stop=f == FC - 1)
                    last.then_inc(dn_full, 1)

            def body(i, q, first):
                up(i, q, 0, first)
                if not first:
                    down(i if q else i - 1, 1 - q, 1)
                up(i, q, 1, first)
                down(i, q, 0)

            run(pe, body)
            down(NR // 2, 0, 1)



I4 = 704
IC = -(-I4 // 128)
IP = IC * 128
QB = 16
QSTEPS = 16
GRID = ((3.5, 2.5), (1.75, 1.25, 0.75, 0.25))


def quantize(dve, step, base, signs, src, out, buf, free_out=None):
    parts, nb = src.shape[0], src.shape[1]
    am, sc, r, hs = (buf[k][0:parts, 0:nb] for k in ("am", "sc", "r", "hs"))
    v, a, acc, sg = (buf[k][0:parts, 0:nb, :] for k in ("v", "a", "acc", "sg"))
    n = 0

    def link(ins):
        nonlocal n
        n += 1
        ins.then_inc(step, 1)
        dve.wait_ge(step, base + n)

    def wide(x):
        return x[:, :, None].to_broadcast([parts, nb, QB])

    link(dve.tensor_reduce(am, src, AXX, ALU.max, apply_absolute_value=True))
    link(dve.tensor_scalar(sc, am, 1.0 / 6.0, 1e-12, ALU.mult, ALU.max))
    link(dve.reciprocal(r, sc))
    link(dve.tensor_tensor(v, src, wide(r), ALU.mult))
    link(dve.scalar_tensor_tensor(a, v, -1.0, v, ALU.mult, ALU.max))
    link(dve.tensor_scalar(hs, sc, 0.5, None, ALU.mult))
    link(dve.tensor_scalar(acc, a, 5.0, 2.0, ALU.is_gt, ALU.mult))
    for mids in GRID:
        for mid in mids:
            link(dve.scalar_tensor_tensor(acc, a, mid, acc, ALU.is_gt, ALU.add))
        if mids is GRID[0]:
            link(dve.tensor_scalar(acc, acc, 2.0, None, ALU.mult))
    dve.wait_ge(*signs)
    link(dve.tensor_tensor(acc, acc, sg, ALU.mult))
    if free_out:
        free_out()
    link(dve.tensor_tensor(out, acc, wide(hs), ALU.mult))
    assert n == QSTEPS


def fp4_mlp(nc, g, n, w):
    tag = f"f{n}_"
    with nc.cleanup_on_exit(), ExitStack() as ctx:
        def sb(name, shape, dt=F32):
            return ctx.enter_context(nc.sbuf_tensor(tag + name, shape, dt))

        def sem(name):
            return nc.alloc_semaphore(tag + name)

        wgu = sb("wgu", [128, 2 * IC, D])
        wdn = sb("wdn", [128, KC, IP])
        wguT = sb("wguT", [128, KC, 2 * IC * 128])
        wdT = sb("wdT", [128, IC, D])
        NBMAX = 3 * D // QB
        buf = {k: sb("q_" + k, [128, NBMAX]) for k in ("am", "sc", "r", "hs")}
        buf |= {k: sb("q_" + k, [128, NBMAX, QB]) for k in ("v", "a", "acc", "sg")}
        xq, xqT = sb("xq", [128, D]), sb("xqT", [128, KC, 128])
        sg, h, hq = sb("sg", [128, I4]), sb("h", [128, I4]), sb("hq", [128, IP])
        hqT = sb("hqT", [128, IC, 128])

        w_in, step, signs, pad = sem("w_in"), sem("step"), sem("signs"), sem("pad")
        wt_full, wt_out = sem("wt_full"), sem("wt_out")
        tx_full, tx_out, up_full, sg_out = sem("tx_full"), sem("tx_out"), sem("up_full"), sem("sg_out")
        th_full, th_out, dn_full, x_done = sem("th_full"), sem("th_out"), sem("dn_full"), sem("x_done")

        PIECES = 6
        HALF = I4 // 2
        PRE = QSTEPS * (PIECES + 1)
        PER = 2 * QSTEPS + 2

        def blocks(x):
            return x.rearrange("p (n b) -> p n b", b=QB)

        def piece(k):
            if k < 4:
                return wgu[:, 3 * k:3 * k + 3, :].rearrange("p t (n b) -> p (t n) b", b=QB)
            return blocks(wdn[:, k - 4, :])

        def run(eng, body):
            body(0, True)
            with eng.Fori(0, NT - 2) as i:
                body(i + 1, True)
            body(NT - 1, False)

        def later(t, k=1):
            return not (isinstance(t, int) and t < k)

        block = ctx.enter_context(nc.Block())

        @block.sync
        def _(sp):
            sp.dma_start(wgu[:, :, :], w["gu"]).then_inc(w_in, 16)
            sp.dma_start(wdn[:, :, :], w["down"]).then_inc(w_in, 16)

        @block.scalar
        def _(act):
            ln_scalar(act, g, n)

            def sign(at, nb):
                act.wait_ge(step, at + 4)
                act.activation(buf["sg"][:, 0:nb, :], buf["v"][:, 0:nb, :], ACT.Sign).then_inc(signs, 1)

            for k in range(PIECES):
                sign(QSTEPS * k, NBMAX)
                for c in (0, 1):
                    act.wait_ge(wt_full, 2 * k + c + 1)
                    pt = g.P[2 * (k % 2) + c]
                    if k < 4:
                        act.activation(wguT[:, c, 384 * k:384 * k + 384], pt[:, 0:384], ACT.Copy).then_inc(wt_out, 1)
                    else:
                        d = k - 4
                        act.activation(wdT[:, 3 * c:3 * c + 3, 128 * d:128 * d + 128],
                                       pt[:, 0:384].rearrange("p (f n) -> p f n", f=3), ACT.Copy).then_inc(wt_out, 1)
            sign(QSTEPS * PIECES, D // QB)
            act.wait_ge(tx_full, 1)
            act.activation(xqT[:, :, :], g.P[4][:, 0:D].rearrange("p (c n) -> p c n", c=KC), ACT.Copy).then_inc(tx_out, 1)

            def silu(t):
                for k in (0, 1):
                    act.wait_ge(up_full, 4 * t + k + 1)
                    if k == 0 and later(t):
                        act.wait_ge(step, PRE + PER * t - QSTEPS)
                    act.activation(sg[:, HALF * k:HALF * k + HALF], g.P[k][:, 0:HALF], ACT.Silu).then_inc(sg_out, 1)

            silu(0)

            def body(t, ahead):
                x = QSTEPS if ahead else 0
                if ahead:
                    sign(PRE + PER * t, D // QB)
                    act.wait_ge(tx_full, t + 2)
                    act.activation(xqT[:, :, :], g.P[4][:, 0:D].rearrange("p (c n) -> p c n", c=KC), ACT.Copy)\
                       .then_inc(tx_out, 1)
                sign(PRE + PER * t + x + 2, I4 // QB)
                for c in (0, 1):
                    act.wait_ge(th_full, 2 * t + c + 1)
                    if c == 0 and later(t):
                        act.wait_ge(dn_full, t)
                    act.activation(hqT[:, 3 * c:3 * c + 3, :], g.P[5 + c][:, 0:384].rearrange("p (f n) -> p f n", f=3),
                                   ACT.Copy).then_inc(th_out, 1)
                if ahead:
                    silu(t + 1)

            run(act, body)

        @block.vector
        def _(dve):
            ln_vector(dve, g, n)
            dve.memset(hq[:, I4:IP], 0.0).then_inc(pad, 1)
            dve.wait_ge(w_in, 32)
            for k in range(PIECES):
                quantize(dve, step, QSTEPS * k, (signs, k + 1), piece(k), piece(k), buf)
            dve.wait_ge(g.sems["xn"], NT * (n + 1))
            quantize(dve, step, QSTEPS * PIECES, (signs, PIECES + 1), blocks(g.XN[:, 0, :]), blocks(xq[:, :]), buf)

            def add(t):
                dve.wait_ge(dn_full, t + 1)
                x = g.X[:, bass.ds(t, 1), :]
                dve.tensor_tensor(x, x, g.P[7][:, None, 0:D], ALU.add).then_inc(x_done, 1)

            def body(t, ahead):
                base = PRE + PER * t
                if ahead:
                    quantize(dve, step, base, (signs, PIECES + 2 + 2 * t),
                             g.XN[:, bass.ds(t + 1, 1), :].rearrange("p a (n b) -> p (a n) b", b=QB), blocks(xq[:, :]), buf,
                             lambda: dve.wait_ge(tx_full, t + 1))
                    base = base + QSTEPS
                if later(t):
                    add(t - 1)
                for k in (0, 1):
                    dve.wait_ge(sg_out, 2 * (t + 1))
                    dve.wait_ge(up_full, 4 * (t + 1))
                    dve.tensor_tensor(h[:, HALF * k:HALF * k + HALF], sg[:, HALF * k:HALF * k + HALF],
                                      g.P[2 + k][:, 0:HALF], ALU.mult).then_inc(step, 1)
                dve.wait_ge(step, base + 2)
                quantize(dve, step, base + 2, (signs, PIECES + 2 + 2 * t + (1 if ahead else 0)),
                         blocks(h[:, :]), blocks(hq[:, 0:I4]), buf,
                         (lambda: dve.wait_ge(th_full, 2 * t)) if later(t) else None)

            run(dve, body)
            add(NT - 1)

        @block.tensor
        def _(pe):
            ln_tensor(pe, g, n)
            xnt_ready(pe, g, n)
            for k in range(PIECES):
                pe.wait_ge(step, QSTEPS * (k + 1))
                for c in (0, 1):
                    if k >= 2:
                        pe.wait_ge(wt_out, 2 * (k - 2) + c + 1)
                    pt = g.P[2 * (k % 2) + c]
                    for f in range(3):
                        if k < 4:
                            last = pe.transpose(pt[:, 128 * f:128 * f + 128], wgu[:, 3 * k + f, 128 * c:128 * c + 128], g.ident[:, :])
                        else:
                            fc = 3 * c + f
                            last = pe.transpose(pt[:, 128 * f:128 * f + 128],
                                                wdn[:, k - 4, 128 * fc:128 * fc + 128], g.ident[:, :])
                    last.then_inc(wt_full, 1)

            def transpose_x():
                for c in range(KC):
                    last = pe.transpose(g.P[4][:, 128 * c:128 * c + 128], xq[:, 128 * c:128 * c + 128], g.ident[:, :])
                last.then_inc(tx_full, 1)

            def up(t):
                pe.wait_ge(tx_out, t + 1)
                for k in range(4):
                    if later(t):
                        if k < 2:
                            pe.wait_ge(sg_out, 2 * t)
                        else:
                            pe.wait_ge(step, PRE + PER * t - QSTEPS)
                    at = IC * 128 * (k // 2) + HALF * (k % 2)
                    for c in range(KC):
                        last = pe.matmul(g.P[k][:, 0:HALF], xqT[:, c, :], wguT[:, c, at:at + HALF], start=c == 0, stop=c == KC - 1)
                    last.then_inc(up_full, 1)

            pe.wait_ge(pad, 1)
            pe.wait_ge(step, PRE)
            transpose_x()
            pe.wait_ge(wt_out, 2 * PIECES)
            up(0)

            def body(t, ahead):
                x = QSTEPS if ahead else 0
                if ahead:
                    pe.wait_ge(step, PRE + PER * t + QSTEPS)
                    transpose_x()
                    pe.wait_ge(step, PRE + PER * t + QSTEPS + 2)
                    up(t + 1)
                pe.wait_ge(step, PRE + PER * t + x + 2 + QSTEPS)
                for c in (0, 1):
                    if later(t):
                        pe.wait_ge(th_out, 2 * t)
                    for f in range(3):
                        fc = 3 * c + f
                        last = pe.transpose(g.P[5 + c][:, 128 * f:128 * f + 128],
                                            hq[:, 128 * fc:128 * fc + 128], g.ident[:, :])
                    last.then_inc(th_full, 1)
                pe.wait_ge(th_out, 2 * (t + 1))
                if later(t):
                    pe.wait_ge(x_done, t)
                for fc in range(IC):
                    last = pe.matmul(g.P[7][:, 0:D], hqT[:, fc, :], wdT[:, fc, :],
                                     start=fc == 0, stop=fc == IC - 1)
                last.then_inc(dn_full, 1)

            run(pe, body)



HP = H // 2
DK = 64
LV = 6
RDL = 64


class Steps:

    def __init__(self, sem, names):
        self.sem, self.names, self.at = sem, list(names), 0

    def reached(self, name, tile):
        return len(self.names) * tile + self.names.index(name) + 1

    def mark(self, ins, name):
        assert self.names[self.at] == name, (self.names[self.at], name)
        self.at = (self.at + 1) % len(self.names)
        ins.then_inc(self.sem, 1)


def delta_rule(nc, g, n, w):
    tag = f"d{n}_"
    with nc.cleanup_on_exit(), ExitStack() as ctx:
        def sb(name, shape, dt=F32):
            return ctx.enter_context(nc.sbuf_tensor(tag + name, shape, dt))

        def sem(name):
            return nc.alloc_semaphore(tag + name)

        T2 = 2 * HP * S
        wqk, wv, wa = sb("wqk", [128, KC, 2, H * DK]), sb("wv", [128, KC, H * DK]), sb("wa", [128, KC, H * DK])
        wout = sb("wout", [128, HP, D])
        u1, u2, wb = sb("u1", [128, KC, RDL]), sb("u2", [RDL, D]), sb("wb", [128, KC, H])
        nw, cw, cb = sb("nw", [128, KC]), sb("cw", [128, KC, 4]), sb("cb", [128, KC])
        u1b, u2b, bb, ab = sb("u1b", [RDL, 1]), sb("u2b", [128, D]), sb("bb", [128, H]), sb("ab", [128, HP])
        hnw, eps = sb("hnw", [128, HP]), sb("eps", [128, 1])
        idq, bones = sb("idq", [128, S]), sb("bones", [128, 128])
        bdm = sb("bdm", [128, 2])
        idb, idqb = sb("idb", [128, 128], BF16), sb("idqb", [128, S], BF16)
        cm, pm, dm = sb("cm", [128, LV, S // 2]), sb("pm", [128, LV, S // 2], U8), sb("dm", [128, S])
        gate, beta = sb("gate", [128, NT, D]), sb("beta", [128, NT, H])
        st, mv = sb("st", [128, NT, 6]), sb("mv", [128, NT, 2])
        ms, sd, rs = sb("ms", [128, NT]), sb("sd", [128, NT]), sb("rs", [128, NT])
        hct = sb("hct", [128, KC, 128])
        at = sb("at", [128, 2, HP, S])
        Tl = [at] + [sb(f"T{k}", [128, 2, HP, S >> k]) for k in range(1, LV)]
        KQ = sb("KQ", [128, 2, HP, 2, S])
        KB = sb("KB", [128, 2, HP, 2, S])
        C = [sb(f"C{k}", [128, 2, HP, 2, S]) for k in range(LV)]
        XX = sb("XX", [128, 2, 2, HP, S])
        X, XT = XX[:, 0], XX[:, 1]
        XTb = sb("XTb", [128, 2, HP, 2, S])
        Y = sb("Y", [128, 2, HP, S])
        YB = sb("YB", [128, 2 * KC * (S + 3) * HP])
        Yb = YB[:, 0:2048].rearrange("p (f h e s) -> p f h e s", f=2, h=HP, e=2)
        N = sb("N", [128, 2, HP, S])
        V = sb("V", [128, 2, HP, DK])
        yT = sb("yT", [128, HP, 2, S])
        ssq, nrm = sb("ssq", [128, 2, H]), sb("nrm", [128, 3, H])
        hz = KQ[:, :, :, :, :].rearrange("p f h k s -> p (f h k s)").rearrange("p (t n) -> p t n", t=NT)
        conv_in = YB[:, :].rearrange("p (c b s) -> p c b s", c=KC, b=B)
        conv = XX[:, :, :, :, :].rearrange("p c f h s -> p c (f h s)")
        g1T = yT[0:RDL, :, :, :].rearrange("p h f s -> p (h f s)")
        hcT = g.XNT

        def nat(x):
            return x.rearrange("p f h s -> p (f h) s")

        qn, kn, kbn, sq = nat(X), nat(XT), nat(Y), nat(N)
        sqk = yT[:, :, :, :].rearrange("p h f s -> p (h f) s")
        NLD = 24

        w_in = sem("w_in")
        bn, ms_done, sd_done, rs_done, hz_done = sem("bn"), sem("ms_done"), sem("sd_done"), sem("rs_done"), sem("hz_done")
        ht_full, ht_out, conv_done, hc_done = sem("ht_full"), sem("ht_out"), sem("conv_done"), sem("hc_done")
        g1_full, g1_out, g2_full, g2_add, g2_out = sem("g1_full"), sem("g1_out"), sem("g2_full"), sem("g2_add"), sem("g2_out")
        b_full, b_add, b_out = sem("b_full"), sem("b_add"), sem("b_out")
        setup, zeroed, pool_zeroed = sem("setup"), sem("zeroed"), sem("pool_zeroed")

        F = (0, 1)
        PE = Steps(sem("pe_steps"), ["q", "k", "a", "v"] + ["qT", "kT", "kbT"] + [f"D{f}" for f in F]
                   + [f"M0{f}" for f in F]
                   + [x for l in range(LV) for x in ([f"Y{l}{f}" for f in F] + ([f"M{l + 1}{f}" for f in F] if l < LV - 1 else [])
                                                     + ([f"G{l}{f}" for f in F] if 0 < l < LV - 1 else [])
                                                     + [f"H{l}{f}" for f in F])]
                   + [f"U{f}" for f in F] + [f"O{f}" for f in F] + [f"S{f}" for f in F] + ["W"])
        AC = Steps(sem("act_steps"), ["q", "k", "qq", "kk", "nrm", "a", "v", "qT", "kbT"]
                   + [x for l in range(LV) for x in ([f"Y{l}{f}" for f in F]
                                                     + ([f"X{l}{f}" for f in F] if 0 < l < LV - 1 else [])
                                                     + [x for f in F for x in ([f"XT{l}{f}"] if l < LV - 1 else []) + [f"XB{l}{f}"]])]
                   + [f"U{f}" for f in F] + [x for f in F for x in (f"O{f}", f"OO{f}")] + [f"rs{f}" for f in F])
        DV = Steps(sem("dve_steps"), ["ssq", "ssk", "eps", "r", "rb", "qn", "kb", "kn", "KP", "QP", "T1"] + [f"D{f}" for f in F]
                   + [x for l in range(LV) for x in [y for f in F for y in ([f"C{l}{f}", f"N{l}{f}"]
                                                                         + ([f"K{l}{f}", f"Q{l}{f}", f"S{l}{f}"] if l < LV - 1 else []))]
                      + ([f"T{l + 2}"] if l < LV - 2 else [])]
                   + [x for f in F for x in (f"r{f}", f"y{f}")] + ["g", "out"])
        PO = Steps(sem("pool_steps"), ["hct"] + [f"Y{l}{f}" for l in range(LV) for f in F])

        def odd(x, m):
            return x.rearrange("p h (n o m) -> p h n o m", o=2, m=m)[:, :, :, 1, :]

        def even(x, m):
            return x.rearrange("p h (n o m) -> p h n o m", o=2, m=m)[:, :, :, 0, :]

        def banks2(k):
            return g.PS[:, k:k + 2, :].rearrange("p a n -> p (a n)")

        block = ctx.enter_context(nc.Block())

        @block.sync
        def _(sp):
            loads = ((wqk[:, :, :, :], w["qk"]), (wv[:, :, :], w["v"]), (wa[:, :, :], w["alpha"]), (wout[:, :, :], w["out"]),
                     (u1[:, :, :], w["u1"]), (u2[:, :], w["u2"]), (wb[:, :, :], w["beta"]), (nw[:, :], w["nw"]),
                     (cw[:, :, :], w["cw"]), (cb[:, :], w["cb"]), (u1b[:, :], w["u1b"]), (u2b[:, :], w["u2b"]),
                     (bb[:, :], w["bb"]), (ab[:, :], w["ab"]), (hnw[:, :], w["hnw"]), (eps[:, :], g.c["eps6"]),
                     (idq[:, :], g.c["idq"]), (bones[:, :], g.c["bones"]), (cm[:, :, :], g.c["cm"]), (dm[:, :], g.c["dm"]),
                     (pm[:, :, :], g.c["pm"]), (bdm[:, :], g.c["bdm"]))
            assert len(loads) == NLD - 2
            for dst, src in loads:
                sp.dma_start(dst, src).then_inc(w_in, 16)

        WIN = 16 * (NLD - 2)

        @block.gpsimd
        def _(pool):
            for k in range(LV):
                pool.memset(C[k][:, :, :, :, :], 0.0).then_inc(pool_zeroed, 1)
            pool.memset(KB[:, :, :, :, :], 0.0).then_inc(pool_zeroed, 1)
            pool.memset(XTb[:, :, :, :, :], 0.0).then_inc(pool_zeroed, 1)
            pool.wait_ge(w_in, WIN)
            pool.wait_ge(hc_done, KC)
            pool.wait_ge(zeroed, 1)
            with pool.Fori(0, NT) as t:
                pool.wait_ge(PE.sem, len(PE.names) * t)
                pool.wait_ge(zeroed, 1)
                PO.mark(pool.tensor_copy(hct[:, :, :], hcT[:, :, bass.ds(128 * t, 128)]), "hct")
                for l in range(LV):
                    for f in F:
                        pool.wait_ge(AC.sem, AC.reached(f"Y{l}{f}", t))
                        PO.mark(pool.tensor_tensor(Yb[:, f, :, :, :], Y[:, f, :, None, :].to_broadcast([128, HP, 2, S]),
                                                   bdm[:, None, :, None].to_broadcast([128, HP, 2, S]), ALU.mult), f"Y{l}{f}")

        @block.scalar
        def _(act):
            ln_scalar(act, g, n)
            act.wait_ge(w_in, WIN)
            act.wait_ge(ms_done, 2)
            act.activation(sd[:, :], rs[:, :], ACT.Sqrt).then_inc(sd_done, 1)
            for t in F:
                act.wait_ge(g1_full, t + 1)
                act.activation(g1T[:, 512 * t:512 * t + 512], g.P[4 + t][0:RDL, :], ACT.Silu, bias=u1b[:, :]).then_inc(g1_out, 1)
            for k in range(4):
                act.wait_ge(ht_full, k + 1)
                for c in range(KC):
                    if k == 0 and c == 0:
                        act.wait_ge(setup, 1)
                    act.activation(conv_in[:, c, 4 * k:4 * k + 4, 3:S + 3],
                                   g.P[k][:, 256 * c:256 * c + 256].rearrange("p (b s) -> p b s", b=4),
                                   ACT.Copy, scale=nw[:, c:c + 1]).then_inc(ht_out, 1)
            for c in range(KC):
                act.wait_ge(conv_done, 4 * (c + 1))
                if c == 0:
                    act.wait_ge(g1_full, 2)
                act.activation(hcT[:, c, :], conv[:, c, :], ACT.Silu, bias=cb[:, c:c + 1]).then_inc(hc_done, 1)
            act.wait_ge(g2_add, 4)
            act.activation(gate[:, :, :], gate[:, :, :], ACT.Sigmoid).then_inc(g2_out, 1)
            act.wait_ge(b_add, 1)
            act.activation(beta[:, :, :], beta[:, :, :], ACT.Sigmoid).then_inc(b_out, 1)

            with act.Fori(0, NT) as t:
                def pe(name):
                    act.wait_ge(PE.sem, PE.reached(name, t))

                def dv(name):
                    act.wait_ge(DV.sem, DV.reached(name, t))

                pe("q")
                act.wait_ge(DV.sem, len(DV.names) * t)
                AC.mark(act.activation(qn, banks2(0).rearrange("p (h d) -> p h d", h=H), ACT.Copy), "q")
                pe("k")
                AC.mark(act.activation(kn, banks2(2).rearrange("p (h d) -> p h d", h=H), ACT.Copy), "k")
                act.wait_ge(AC.sem, AC.reached("k", t))
                AC.mark(act.activation(sq, qn, ACT.Square), "qq")
                AC.mark(act.activation(sqk, kn, ACT.Square), "kk")
                dv("ssk")
                AC.mark(act.activation(nrm[:, 0:2, :], ssq[:, :, :], ACT.Sqrt), "nrm")
                pe("a")
                for hp in range(HP):
                    ins = act.activation(at[:, :, hp, :], g.P[6 + hp // 4][:, 128 * (hp % 4):128 * (hp % 4) + 128]
                                         .rearrange("p (f s) -> p f s", f=2), ACT.Sigmoid, bias=ab[:, hp:hp + 1])
                AC.mark(ins, "a")
                pe("v")
                AC.mark(act.activation(V[:, :, :, :], g.PS[:, 4:6, :].rearrange("p f (h d) -> p f h d", h=HP), ACT.Copy), "v")
                pe("qT")
                AC.mark(act.activation(KQ[:, :, :, 1, :], banks2(0).rearrange("p (h f s) -> p f h s", h=HP, f=2), ACT.Copy), "qT")
                pe("kbT")
                for e in F:
                    rows = slice(64 * e, 64 * e + 64)
                    ins = act.activation(KB[rows, :, :, e, :], banks2(4)[rows, :].rearrange("p (h f s) -> p f h s", h=HP, f=2), ACT.Copy)
                AC.mark(ins, "kbT")

                def block_diagonal(dst, bank):
                    for e in F:
                        rows = slice(64 * e, 64 * e + 64)
                        ins = act.activation(dst[rows, :, e, :], bank[rows, :].rearrange("p (h s) -> p h s", h=HP), ACT.Copy)
                    return ins

                for l in range(LV):
                    for f in F:
                        pe(f"Y{l}{f}")
                        AC.mark(act.activation(Y[:, f, :, :], g.P[2 + f].rearrange("p (h s) -> p h s", h=HP), ACT.Copy), f"Y{l}{f}")
                    if 0 < l < LV - 1:
                        for f in F:
                            pe(f"G{l}{f}")
                            AC.mark(act.activation(X[:, f, :, :], g.P[4 + f].rearrange("p (h s) -> p h s", h=HP), ACT.Copy), f"X{l}{f}")
                    for f in F:
                        pe(f"H{l}{f}")
                        if l < LV - 1:
                            AC.mark(act.activation(XT[:, f, :, :], g.P[6 + f].rearrange("p (h s) -> p h s", h=HP), ACT.Copy), f"XT{l}{f}")
                        AC.mark(block_diagonal(XTb[:, f], g.P[6 + f]), f"XB{l}{f}")
                for f in F:
                    pe(f"U{f}")
                    AC.mark(block_diagonal(Yb[:, f], g.P[2 + f]), f"U{f}")
                for f in F:
                    pe(f"O{f}")
                    AC.mark(act.activation(X[:, f, :, :], g.P[4 + f].rearrange("p (h s) -> p h s", h=HP), ACT.Copy), f"O{f}")
                    AC.mark(act.activation(XT[:, f, :, :], g.P[4 + f].rearrange("p (h s) -> p h s", h=HP), ACT.Square), f"OO{f}")
                for f in F:
                    pe(f"S{f}")
                    AC.mark(act.activation(Y[:, f, :, :], g.P[6 + f].rearrange("p (h s) -> p h s", h=HP), ACT.Sqrt, bias=eps[:, :]), f"rs{f}")

        @block.vector
        def _(dve):
            ln_vector(dve, g, n)
            dve.memset(conv_in[:, :, :, 0:3], 0.0).then_inc(setup, 1)
            dve.wait_ge(g.sems["xn"], NT * (n + 1))
            for t in range(NT):
                dve.bn_stats(st[:, t, :], g.XN[:, t, :]).then_inc(bn, 1)
            dve.wait_ge(bn, NT)
            for t in range(NT):
                dve.bn_aggr(mv[:, t, :], st[:, t, :]).then_inc(bn, 1)
            dve.wait_ge(bn, 2 * NT)
            dve.tensor_tensor(ms[:, :], mv[:, :, 0], mv[:, :, 0], ALU.mult).then_inc(ms_done, 1)
            dve.wait_ge(ms_done, 1)
            dve.scalar_tensor_tensor(rs[:, :], ms[:, :], 1e-6, mv[:, :, 1], ALU.add, ALU.add).then_inc(ms_done, 1)
            dve.wait_ge(sd_done, 1)
            dve.reciprocal(rs[:, :], sd[:, :]).then_inc(rs_done, 1)
            dve.wait_ge(rs_done, 1)
            for t in range(NT):
                dve.tensor_scalar(hz[:, t, :], g.XN[:, t, :], rs[:, t:t + 1], None, ALU.mult).then_inc(hz_done, 1)
            dve.wait_ge(w_in, WIN)
            dve.tensor_copy(idb[:, :], g.ident[:, :]).then_inc(setup, 1)
            dve.tensor_copy(idqb[:, :], idq[:, :]).then_inc(setup, 1)
            dve.tensor_tensor(wout[:, :, :], wout[:, :, :], hnw[:, :, None].to_broadcast([128, HP, D]), ALU.mult).then_inc(setup, 1)
            dve.wait_ge(ht_out, 4 * KC)
            for c in range(KC):
                out = conv[:, c, :].rearrange("p (b s) -> p b s", b=B)
                dve.tensor_scalar(out, conv_in[:, c, :, 0:S], cw[:, c, 0:1], None, ALU.mult).then_inc(conv_done, 1)
                for k in range(1, 4):
                    dve.wait_ge(conv_done, 4 * c + k)
                    dve.scalar_tensor_tensor(out, conv_in[:, c, :, k:k + S], cw[:, c, k:k + 1], out, ALU.mult, ALU.add)\
                       .then_inc(conv_done, 1)
            dve.wait_ge(conv_done, 4 * KC)
            dve.memset(YB[:, :], 0.0).then_inc(zeroed, 1)
            for k in range(4):
                dve.wait_ge(g2_full, k + 1)
                dve.tensor_tensor(gate[:, 2 * k:2 * k + 2, :], g.P[k].rearrange("p (t n) -> p t n", t=2),
                                  u2b[:, None, :].to_broadcast([128, 2, D]), ALU.add).then_inc(g2_add, 1)
            dve.wait_ge(b_full, 1)
            dve.tensor_tensor(beta[:, :, :], g.P[6][:, 0:NT * H].rearrange("p (t h) -> p t h", t=NT),
                              bb[:, None, :].to_broadcast([128, NT, H]), ALU.add).then_inc(b_add, 1)
            dve.wait_ge(g2_out, 1)
            dve.wait_ge(b_out, 1)
            dve.wait_ge(pool_zeroed, LV + 2)

            with dve.Fori(0, NT) as t:
                def after(steps, name):
                    dve.wait_ge(steps.sem, steps.reached(name, t))

                after(AC, "qq")
                DV.mark(dve.reduce_sum(ssq[:, 0, :], sq, AXX), "ssq")
                after(AC, "kk")
                DV.mark(dve.reduce_sum(ssq[:, 1, :], sqk, AXX), "ssk")
                after(AC, "nrm")
                DV.mark(dve.tensor_scalar(nrm[:, 0:2, :], nrm[:, 0:2, :], 1e-6, None, ALU.add), "eps")
                after(DV, "eps")
                DV.mark(dve.reciprocal(nrm[:, 0:2, :], nrm[:, 0:2, :]), "r")
                after(DV, "r")
                DV.mark(dve.tensor_tensor(nrm[:, 2:3, :], nrm[:, 1:2, :], beta[:, bass.ds(t, 1), :], ALU.mult), "rb")
                DV.mark(dve.tensor_tensor(qn, qn, nrm[:, 0, :, None].to_broadcast([128, H, DK]), ALU.mult), "qn")
                after(DV, "rb")
                DV.mark(dve.tensor_tensor(kbn, kn, nrm[:, 2, :, None].to_broadcast([128, H, DK]), ALU.mult), "kb")
                after(DV, "kb")
                DV.mark(dve.tensor_tensor(kn, kn, nrm[:, 1, :, None].to_broadcast([128, H, DK]), ALU.mult), "kn")
                after(PE, "kT")
                after(AC, "a")
                DV.mark(dve.tensor_tensor(KQ[:, :, :, 0, :], banks2(2).rearrange("p (h f s) -> p f h s", h=HP, f=2),
                                          at[:, :, :, :], ALU.mult), "KP")
                after(PE, "D1")
                DV.mark(dve.tensor_tensor(KQ[:, :, :, 1, :], KQ[:, :, :, 1, :], at[:, :, :, :], ALU.mult), "QP")

                def products(l):
                    src = Tl[l][:, :, :, :].rearrange("p f h (n o) -> p (f h) n o", o=2)
                    DV.mark(dve.tensor_tensor(Tl[l + 1][:, :, :, :].rearrange("p f h n -> p (f h) n"), src[:, :, :, 0],
                                              src[:, :, :, 1], ALU.mult), f"T{l + 1}")

                products(0)
                for f in F:
                    after(PE, f"D{f}")
                    DV.mark(dve.tensor_tensor(N[:, f, :, :], g.P[6 + f].rearrange("p (h s) -> p h s", h=HP),
                                              dm[:, None, :].to_broadcast([128, HP, S]), ALU.mult), f"D{f}")
                after(DV, "D1")
                for l in range(LV):
                    m = 1 << l
                    nb = S // (2 * m)
                    for f in F:
                        after(PE, f"M{l}{f}")
                        got = g.P[f].rearrange("p (h k n m) -> p h k n m", h=HP, k=2, m=m)
                        for e in F:
                            rows = slice(64 * e, 64 * e + 64)
                            mask = cm[rows, l, :].rearrange("p (n m) -> p n m", m=m)
                            ins = dve.tensor_tensor(odd(C[l][rows, f, :, e, :], m), got[rows, :, 0],
                                                    mask[:, None, :, :].to_broadcast([64, HP, nb, m]), ALU.mult)
                        DV.mark(ins, f"C{l}{f}")
                        mask = pm[:, l, :].rearrange("p (n m) -> p n m", m=m)
                        DV.mark(dve.copy_predicated(odd(N[:, f, :, :], m),
                                                    mask[:, None, :, :].to_broadcast([128, HP, nb, m]), got[:, :, 1]), f"N{l}{f}")
                        if l < LV - 1:
                            if f == 0:
                                after(DV, f"T{l + 1}")
                                if l == 0:
                                    after(DV, "QP")
                            total = Tl[l][:, f, :, :].rearrange("p h (n o) -> p h n o", o=2)
                            for k, name in ((0, "K"), (1, "Q")):
                                x = odd(KQ[:, f, :, k, :], m)
                                DV.mark(dve.tensor_tensor(x, x, total[:, :, :, 0, None].to_broadcast([128, HP, nb, m]), ALU.mult),
                                        f"{name}{l}{f}")
                            for e in F:
                                rows = slice(64 * e, 64 * e + 64)
                                x = even(KB[rows, f, :, e, :], m)
                                ins = dve.tensor_tensor(x, x, total[rows, :, :, 1, None].to_broadcast([64, HP, nb, m]), ALU.mult)
                            DV.mark(ins, f"S{l}{f}")
                    if l < LV - 2:
                        products(l + 1)
                for f in F:
                    after(AC, f"rs{f}")
                    DV.mark(dve.reciprocal(Y[:, f, :, :], Y[:, f, :, :]), f"r{f}")
                    after(DV, f"r{f}")
                    DV.mark(dve.tensor_tensor(yT[:, :, f, :], X[:, f, :, :], Y[:, f, :, :], ALU.mult), f"y{f}")
                after(PE, "W")
                gt = gate[:, bass.ds(t, 1), :]
                DV.mark(dve.tensor_tensor(gt, gt, g.P[0][:, None, 0:D], ALU.mult), "g")
                after(DV, "g")
                y = g.XN[:, bass.ds(t, 1), :]
                DV.mark(dve.tensor_tensor(y, y, gt, ALU.add), "out")

        @block.tensor
        def _(pe):
            ln_tensor(pe, g, n)
            pe.wait_ge(w_in, WIN)
            xnt_ready(pe, g, n)
            for t in F:
                for c in range(KC):
                    last = pe.matmul(g.P[4 + t][0:RDL, :], u1[:, c, :], g.XNT[:, c, 512 * t:512 * t + 512], start=c == 0, stop=c == KC - 1)
                last.then_inc(g1_full, 1)
            for k in range(4):
                pe.wait_ge(hz_done, 2 * k + 2)
                for c in range(KC):
                    for t in F:
                        last = pe.transpose(g.P[k][:, 256 * c + 128 * t:256 * c + 128 * t + 128],
                                            hz[:, 2 * k + t, 128 * c:128 * c + 128], g.ident[:, :])
                last.then_inc(ht_full, 1)
            pe.wait_ge(g1_out, 2)
            pe.wait_ge(ht_out, 4 * KC)
            for k in range(4):
                for t in F:
                    last = pe.matmul(g.P[k][:, D * t:D * t + D], g1T[:, 128 * (2 * k + t):128 * (2 * k + t) + 128], u2[:, :],
                                     start=True, stop=True)
                last.then_inc(g2_full, 1)
            pe.wait_ge(hc_done, KC)
            for t in range(NT):
                for c in range(KC):
                    last = pe.matmul(g.P[6][:, H * t:H * t + H], hcT[:, c, 128 * t:128 * t + 128], wb[:, c, :],
                                     start=c == 0, stop=c == KC - 1)
            last.then_inc(b_full, 1)
            pe.wait_ge(g2_add, 4)
            pe.wait_ge(b_add, 1)
            pe.wait_ge(setup, 4)
            pe.wait_ge(pool_zeroed, LV + 2)

            with pe.Fori(0, NT) as t:
                def after(steps, name):
                    pe.wait_ge(steps.sem, steps.reached(name, t))

                after(PO, "hct")
                pe.wait_ge(DV.sem, len(DV.names) * t)
                for k, name in ((0, "q"), (1, "k")):
                    for j in F:
                        for c in range(KC):
                            last = pe.matmul(g.P[2 * k + j], hct[:, c, :], wqk[:, c, k, 512 * j:512 * j + 512],
                                             start=c == 0, stop=c == KC - 1)
                    PE.mark(last, name)
                for hp in range(HP):
                    for c in range(KC):
                        last = pe.matmul(g.P[6 + hp // 4][:, 128 * (hp % 4):128 * (hp % 4) + 128],
                                         wa[:, c, 128 * hp:128 * hp + 128], hct[:, c, :], start=c == 0, stop=c == KC - 1)
                PE.mark(last, "a")
                for f in F:
                    for e in F:
                        for c in range(KC):
                            cols = wv[:, c, :].rearrange("p (h e d) -> p h e d", e=2, d=DK)[:, :, e, :]
                            last = pe.matmul(g.P[4 + f][64 * e:64 * e + 64, :], hct[:, c, 64 * f:64 * f + 64], cols,
                                             start=c == 0, stop=c == KC - 1)
                PE.mark(last, "v")
                for src, bank, ready, name in ((qn, 0, (DV, "qn"), "qT"), (kn, 2, (DV, "kn"), "kT"), (kbn, 4, (AC, "v"), "kbT")):
                    after(*ready)
                    flat = src.rearrange("p h d -> p (h d)")
                    for hp in range(HP):
                        last = pe.transpose(g.P[bank + hp // 4][:, 128 * (hp % 4):128 * (hp % 4) + 128],
                                            flat[:, 128 * hp:128 * hp + 128], g.ident[:, :])
                    PE.mark(last, name)
                after(AC, "kbT")
                for f in F:
                    for hp in range(HP):
                        last = pe.matmul(g.P[6 + f][:, 64 * hp:64 * hp + 64], KB[:, f, hp, :, :].rearrange("p e s -> p (e s)"),
                                         KQ[:, f, hp, 1, :], start=True, stop=True)
                    PE.mark(last, f"D{f}")

                def level_products(l):
                    m = 1 << l
                    for f in F:
                        if l == 0:
                            after(DV, "QP")
                        else:
                            after(DV, f"S{l - 1}{f}")
                        for hp in range(HP):
                            last = pe.matmul(g.P[f][:, 64 * hp:64 * hp + 64], KB[:, f, hp, :, :].rearrange("p e s -> p (e s)"),
                                             odd(KQ[:, f, hp, :, :], m), start=True, stop=True)
                        PE.mark(last, f"M{l}{f}")

                def bd(x):
                    return x.rearrange("p e s -> p (e s)")

                level_products(0)
                for l in range(LV):
                    for f in F:
                        after(DV, f"C{l}{f}")
                        if l == 0 and f == 0:
                            after(DV, "KP")
                        if 1 < l:
                            after(AC, f"X{l - 1}{f}")
                        pe.matmul(g.P[2 + f], idb[:, :], idqb[:, None, :].to_broadcast([128, HP, S]), start=True,
                                  stop=True, skip_group_check=True)
                        for hp in range(HP):
                            x = idq[:, :] if l == 0 else Y[:, f, hp, :] if l == 1 else X[:, f, hp, :]
                            last = pe.matmul(g.P[2 + f][:, 64 * hp:64 * hp + 64], bd(C[l][:, f, hp, :, :]), x,
                                             start=False, stop=True, skip_group_check=True)
                        PE.mark(last, f"Y{l}{f}")
                    if l < LV - 1:
                        level_products(l + 1)
                    if 0 < l < LV - 1:
                        for f in F:
                            after(AC, f"Y{l}{f}")
                            after(AC, f"XB{l - 1}{f}")
                            for hp in range(HP):
                                last = pe.matmul(g.P[4 + f][:, 64 * hp:64 * hp + 64], bd(XTb[:, f, hp, :, :]), Y[:, f, hp, :],
                                                 start=True, stop=True)
                            PE.mark(last, f"G{l}{f}")
                    for f in F:
                        after(PO, f"Y{l}{f}")
                        if l == 0:
                            after(DV, f"D{f}")
                        else:
                            after(AC, f"XB{l - 1}{f}")
                        for hp in range(HP):
                            x = idq[:, :] if l == 0 else XT[:, f, hp, :]
                            last = pe.matmul(g.P[6 + f][:, 64 * hp:64 * hp + 64], bd(Yb[:, f, hp, :, :]), x, start=True, stop=True)
                        PE.mark(last, f"H{l}{f}")
                for f in F:
                    after(AC, f"XB{LV - 1}{f}")
                    for hp in range(HP):
                        last = pe.matmul(g.P[2 + f][:, 64 * hp:64 * hp + 64], bd(XTb[:, f, hp, :, :]), V[:, f, hp, :], start=True, stop=True)
                    PE.mark(last, f"U{f}")
                for f in F:
                    after(AC, f"U{f}")
                    after(DV, f"N{LV - 1}{f}")
                    for hp in range(HP):
                        last = pe.matmul(g.P[4 + f][:, 64 * hp:64 * hp + 64], bd(Yb[:, f, hp, :, :]), N[:, f, hp, :], start=True, stop=True)
                    PE.mark(last, f"O{f}")
                for f in F:
                    after(AC, f"OO{f}")
                    last = pe.matmul(g.P[6 + f], bones[:, :], XT[:, f, :, :].rearrange("p h s -> p (h s)"), start=True, stop=True)
                    PE.mark(last, f"S{f}")
                after(DV, "y1")
                for hp in range(HP):
                    last = pe.matmul(g.P[0][:, 0:D], yT[:, hp, :, :].rearrange("p f s -> p (f s)"), wout[:, hp, :],
                                     start=hp == 0, stop=hp == HP - 1)
                PE.mark(last, "W")



FF = 1024
FFC = FF // 128


def gated_mlp(nc, g, n, w):
    tag = f"g{n}_"
    with nc.cleanup_on_exit(), ExitStack() as ctx:
        def sb(name, shape, dt=F32):
            return ctx.enter_context(nc.sbuf_tensor(tag + name, shape, dt))

        def sem(name):
            return nc.alloc_semaphore(tag + name)

        w1, w3, w2 = sb("w1", [128, KC, FF]), sb("w3", [128, KC, FF]), sb("w2", [128, FFC, D])
        fw = sb("fw", [128, KC])
        st, mv = sb("st", [128, NT, 6]), sb("mv", [128, NT, 2])
        ms, sd, rs = sb("ms", [128, NT]), sb("sd", [128, NT]), sb("rs", [128, NT])
        z = sb("z", [128, NT, D])
        s1, hT = sb("s1", [128, 2, 512]), sb("hT", [128, FFC, NT * 128])
        w_in, bn, ms_done, sd_done, rs_done, z_done = (
            sem("w_in"), sem("bn"), sem("ms_done"), sem("sd_done"), sem("rs_done"), sem("z_done"))
        zt_full, zt_out, xy = sem("zt_full"), sem("zt_out"), sem("xy")
        h1_full, h3_full, s1_out, h_out, o_full, x_done = (
            sem("h1_full"), sem("h3_full"), sem("s1_out"), sem("h_out"), sem("o_full"), sem("x_done"))

        block = ctx.enter_context(nc.Block())

        @block.sync
        def _(sp):
            for dst, src in ((w1[:, :, :], w["w1"]), (w3[:, :, :], w["w3"]), (w2[:, :, :], w["w2"]), (fw[:, :], w["fw"])):
                sp.dma_start(dst, src).then_inc(w_in, 16)

        @block.scalar
        def _(act):
            act.wait_ge(ms_done, 2)
            act.activation(sd[:, :], rs[:, :], ACT.Sqrt).then_inc(sd_done, 1)
            act.wait_ge(w_in, 64)
            for k in range(4):
                act.wait_ge(zt_full, k + 1)
                for c in range(KC):
                    act.activation(g.XNT[:, c, 256 * k:256 * k + 256], g.P[k][:, 256 * c:256 * c + 256], ACT.Copy,
                                   scale=fw[:, c:c + 1]).then_inc(zt_out, 1)
            for k in range(2 * FFC):
                act.wait_ge(h1_full, k + 1)
                if k >= 2:
                    act.wait_ge(h_out, k - 1)
                act.activation(s1[:, k % 2, :], g.P[k % 2], ACT.Silu).then_inc(s1_out, 1)

        @block.vector
        def _(dve):
            for t in range(NT):
                dve.bn_stats(st[:, t, :], g.XN[:, t, :]).then_inc(bn, 1)
            dve.wait_ge(bn, NT)
            for t in range(NT):
                dve.bn_aggr(mv[:, t, :], st[:, t, :]).then_inc(bn, 1)
            dve.wait_ge(bn, 2 * NT)
            dve.tensor_tensor(ms[:, :], mv[:, :, 0], mv[:, :, 0], ALU.mult).then_inc(ms_done, 1)
            dve.wait_ge(ms_done, 1)
            dve.scalar_tensor_tensor(rs[:, :], ms[:, :], 1e-6, mv[:, :, 1], ALU.add, ALU.add).then_inc(ms_done, 1)
            dve.wait_ge(sd_done, 1)
            dve.reciprocal(rs[:, :], sd[:, :]).then_inc(rs_done, 1)
            dve.wait_ge(rs_done, 1)
            for t in range(NT):
                dve.tensor_scalar(z[:, t, :], g.XN[:, t, :], rs[:, t:t + 1], None, ALU.mult).then_inc(z_done, 1)
            dve.tensor_tensor(g.X[:, :, :], g.X[:, :, :], g.XN[:, :, :], ALU.add).then_inc(xy, 1)
            for k in range(2 * FFC):
                dve.wait_ge(s1_out, k + 1)
                dve.wait_ge(h3_full, k + 1)
                dve.tensor_tensor(hT[:, k % FFC, 512 * (k // FFC):512 * (k // FFC) + 512], s1[:, k % 2, :], g.P[2 + k % 2],
                                  ALU.mult).then_inc(h_out, 1)
            dve.wait_ge(xy, 1)
            for t in range(NT):
                dve.wait_ge(o_full, t + 1)
                dve.tensor_tensor(g.X[:, t, :], g.X[:, t, :], g.P[4 + t % 4][:, 0:D], ALU.add).then_inc(x_done, 1)

        @block.tensor
        def _(pe):
            for k in range(4):
                pe.wait_ge(z_done, 2 * k + 2)
                for c in range(KC):
                    for t in (0, 1):
                        last = pe.transpose(g.P[k][:, 256 * c + 128 * t:256 * c + 128 * t + 128],
                                            z[:, 2 * k + t, 128 * c:128 * c + 128], g.ident[:, :])
                last.then_inc(zt_full, 1)
            pe.wait_ge(w_in, 64)
            pe.wait_ge(zt_out, 4 * KC)
            for th in (0, 1):
                for fc in range(FFC):
                    k = FFC * th + fc
                    for bank, wt, full in ((k % 2, w1, h1_full), (2 + k % 2, w3, h3_full)):
                        if k >= 2:
                            pe.wait_ge(h_out, k - 1)
                        for c in range(KC):
                            last = pe.matmul(g.P[bank], wt[:, c, 128 * fc:128 * fc + 128], g.XNT[:, c, 512 * th:512 * th + 512],
                                             start=c == 0, stop=c == KC - 1)
                        last.then_inc(full, 1)
            for t in range(NT):
                pe.wait_ge(h_out, FFC * (t // 4 + 1))
                if t >= 4:
                    pe.wait_ge(x_done, t - 3)
                for fc in range(FFC):
                    last = pe.matmul(g.P[4 + t % 4][:, 0:D], hT[:, fc, 128 * t:128 * t + 128], w2[:, fc, :],
                                     start=fc == 0, stop=fc == FFC - 1)
                last.then_inc(o_full, 1)


def _chunked(w):
    k, m = w.shape
    return np.ascontiguousarray(w.reshape(k // 128, 128, m).transpose(1, 0, 2))


def _grouped(w):
    out = np.zeros(w.shape[:-1] + (3, GR), w.dtype)
    for gg in range(3):
        out[..., gg, 0:GH[gg] * HD] = w[..., 6 * HD * gg:6 * HD * gg + GH[gg] * HD]
    return out


def _spread(w):
    out = np.zeros((4, 32, 4) + w.shape[1:], w.dtype)
    out[:, 0:HD] = np.moveaxis(w.reshape((4, 4, HD) + w.shape[1:]), 0, 2)
    return out.reshape((128, 4) + w.shape[1:])


def _attention_weights(wq, bq, wk, bk, wv, bv, wo, bo):
    def g96(w):
        return np.ascontiguousarray(_grouped(_chunked(w).reshape(128, KC, D)))
    return {
        "wq": g96(wq), "wk": g96(wk), "wv": _chunked(wv), "wo": _spread(wo),
        "bq": np.ascontiguousarray(_grouped(bq[None])[0].T), "bk": np.ascontiguousarray(_grouped(bk[None])[0].T),
        "bv": _spread(bv), "bo": np.tile(bo[None], (128, 1)),
    }


def _constants():
    p = np.arange(128)
    rel = np.clip(p[:, None] - np.arange(S)[None], -2, 2) + 2
    half = np.arange(HR, dtype=np.float32) / np.float32(HR)
    angles = (p[:, None] % S).astype(np.float32) * (np.float32(1) / np.float32(10000) ** half)[None]
    idq = p[:, None] % S == np.arange(S)[None]
    sibling = np.zeros((128, LV, S // 2))
    for lv in range(LV):
        i = np.arange(S).reshape(-1, 2, 1 << lv)[:, 1].reshape(-1)
        sibling[:, lv] = (p[:, None] % S) >> lv == (i[None] >> lv) - 1
    c = {
        "ident": np.eye(128), "hmask": p[:GR, None] // HD == np.arange(6)[None],
        "selden": p[:, None] == 32 * (p[None] // 32) + HD,
        "rmask": np.stack([np.concatenate([(rel == 2 * jj + jp).T for jp in (0, 1)], 0) for jj in (0, 1)], 1),
        "kmask": np.stack([rel == j for j in range(RD)], 1),
        "idq": idq,
        "hmask8": p[:, None] // HD == np.arange(8)[None],
        "causal": np.where(np.arange(S)[None] <= p[:, None] % S, 0.0, NEG),
        "tri": np.tile(np.tril(np.ones((NR, NR)), -1)[None], (128, 1, 1)),
        "eps6": np.full((128, 1), 1e-6), "bones": (p[:, None] // 64 == p[None] // 64) / 64.0,
        "bdm": p[:, None] // 64 == np.arange(2)[None], "dm": idq,
        "cm": -sibling, "cos": np.cos(angles), "sin": np.sin(angles),
    }
    c = {k: np.ascontiguousarray(v).astype(np.float32) for k, v in c.items()}
    return c | {"pm": sibling.astype(bool)}


def _arrays(i):
    a = {"x": i["x"].reshape(NT, 128, D).transpose(1, 0, 2),
         "ctx": i["ctx_1024"].transpose(0, 2, 1).reshape(B, KC, 128, S2).transpose(0, 2, 1, 3)}
    for k, v in _attention_weights(*(i["L0_xattn_" + k] for k in ("Wq", "bq", "Wk", "bk", "Wv", "bv", "Wo", "bo"))).items():
        a["xa0_" + k] = v
    wkv, bkv = i["L1_xattn_Wkv"], i["L1_xattn_bkv"]
    for k, v in _attention_weights(i["L1_xattn_Wq"], i["L1_xattn_bq"], wkv[:, :D], bkv[:D], wkv[:, D:], bkv[D:],
                                   i["L1_xattn_Wout"], i["L1_xattn_bout"]).items():
        a["xa1_" + k] = v
    rk, rv = i["L0_xattn_rel_k"], i["L0_xattn_rel_v"]
    a["rel_k"] = np.tile(rk.T, (GR // HD, 1))
    relv = np.zeros((128, RD + 1, 32), rv.dtype)
    relv[:, :, 0:HD] = rv[None]
    a["rel_v"] = relv
    v4 = np.zeros((4, 32, 1), rv.dtype)
    v4[:, 0:HD, 0] = rv[None, RD]
    a["rel_v4"] = v4.reshape(128, 1)
    for k in ("W_q", "W_dkv"):
        a["la_" + k] = _chunked(i["L0_attn_" + k])
    a["la_W_uk"] = i["L0_attn_W_uk"]
    a["la_W_uv"] = i["L0_attn_W_uv"].reshape(LAT, 4, 2, 2, HD).transpose(0, 1, 3, 2, 4).reshape(LAT, D)
    a["la_W_o"] = _chunked(i["L0_attn_W_o"].reshape(4, 2, 2, HD, D).transpose(0, 2, 1, 3, 4).reshape(D, D))
    a["la_gamma"], a["la_beta"] = (np.tile(i["L0_attn_ln_" + k][None], (128, 1)) for k in ("gamma", "beta"))
    up = np.concatenate([i["L0_ffn_w_up"], i["L0_ffn_shared_w_up"]])
    down = np.concatenate([i["L0_ffn_w_down"], i["L0_ffn_shared_w_down"]])
    a["mo_up"] = up.transpose(0, 2, 1).reshape(E_MOE, KC, 128, F_MOE).transpose(0, 2, 1, 3)
    a["mo_down"] = down.transpose(0, 2, 1).reshape(E_MOE, FC, 128, D).transpose(0, 2, 1, 3)
    a["mo_wr"] = _chunked(i["L0_ffn_router_w"].T)
    a["mo_br"] = np.tile(i["L0_ffn_router_b"][None], (128, 1))
    p5 = {k[8:]: v for k, v in i.items() if k.startswith("L1_attn_")}

    def columns(v):
        return np.moveaxis(v.reshape((KC, 128) + v.shape[1:]), 0, 1)
    a["db_qk"] = np.stack([_chunked(p5["q_w"]), _chunked(p5["k_w"])], 2)
    for k, v in (("v", "v_w"), ("alpha", "alpha_w"), ("out", "out_w"), ("u1", "u1_w"), ("beta", "beta_w"), ("w1", "ff_w1"),
                 ("w3", "ff_w3"), ("w2", "ff_w2")):
        a["db_" + k] = _chunked(p5[v])
    a["db_u2"], a["db_u1b"] = p5["u2_w"], p5["u1_b"][:, None]
    a["db_u2b"], a["db_bb"] = np.tile(p5["u2_b"][None], (128, 1)), np.tile(p5["beta_b"][None], (128, 1))
    a["db_nw"], a["db_cb"], a["db_fw"] = columns(p5["norm_in_w"]), columns(p5["conv_b"]), columns(p5["ff_norm_w"])
    a["db_cw"] = columns(p5["conv_w"][:, 0])
    a["db_ab"], a["db_hnw"] = p5["alpha_b"].reshape(HP, 128).T, p5["head_norm_w"].reshape(HP, 128).T
    gu = np.zeros((2, IC * 128, D), i["L1_ffn_w_gate"].dtype)
    gu[0, :I4], gu[1, :I4] = i["L1_ffn_w_gate"], i["L1_ffn_w_up"]
    a["fp_gu"] = gu.reshape(2 * IC, 128, D).transpose(1, 0, 2)
    a["fp_down"] = np.pad(i["L1_ffn_w_down"], ((0, 0), (0, IP - I4))).reshape(KC, 128, IP).transpose(1, 0, 2)
    m = i["mask_BxS2_bf0"]
    mt = np.zeros((B, NCH * 128), bool)
    mt[:, :S2] = m
    a["mask_T"] = mt.reshape(B, NCH, 128).transpose(2, 0, 1).reshape(128, B * NCH)
    a["mask_row"] = m.reshape(1, B * S2)
    for k, v in _constants().items():
        a["c_" + k] = v
    return {k: np.ascontiguousarray(v) for k, v in a.items()}


def build_program(nc, i, out):
    def group(prefix):
        return {k[len(prefix):]: v for k, v in i.items() if k.startswith(prefix)}

    with ExitStack() as ctx:
        g = Persistent(nc, ctx, group("c_"))
        load_x(nc, g, i["x"])
        cross_attention(nc, g, 0, i["ctx"], group("xa0_"), rel={"k": i["rel_k"], "v": i["rel_v"], "v4": i["rel_v4"]})
        latent_attention(nc, g, 1, group("la_"))
        moe(nc, g, 2, group("mo_"))
        cross_attention(nc, g, 3, i["ctx"], group("xa1_"), mask={"T": i["mask_T"], "row": i["mask_row"]})
        delta_rule(nc, g, 4, group("db_"))
        gated_mlp(nc, g, 4, group("db_"))
        fp4_mlp(nc, g, 5, group("fp_"))
        store_x(nc, g, out)


def kernel(**inputs):
    import concourse.bacc as bacc
    from concourse.bass_utils import run_bass_kernel_spmd

    arrays = _arrays({k: np.asarray(v) for k, v in inputs.items()})
    nc = bacc.Bacc("TRN2", target_bir_lowering=False, num_devices=1)
    aps = {k: nc.dram_tensor(f"in_{k}", v.shape, mybir.dt.from_np(v.dtype), kind="ExternalInput").ap() for k, v in arrays.items()}
    out = nc.dram_tensor("out", (128, NT, D), F32, kind="ExternalOutput").ap()
    build_program(nc, aps, out)
    r = run_bass_kernel_spmd(nc, [{f"in_{k}": v for k, v in arrays.items()}], core_ids=[0])
    y = np.asarray(r.results[0]["out"])
    return y.transpose(1, 0, 2).reshape(B, S, D)
```
